# Optimizing a Trainium2 kernel written in Bass

```python
import numpy as np
import jax
import jax.numpy as jnp

def _softmax(x, axis=-1):
    return jax.nn.softmax(x, axis=axis)

def _gelu(x):
    return jax.nn.gelu(x, approximate=True)

def _silu(x):
    return jax.nn.silu(x)

def _sigmoid(x):
    return jax.nn.sigmoid(x)

def _layernorm(x, axis=-1, eps=1e-05):
    m = jnp.mean(x, axis=axis, keepdims=True)
    v = jnp.var(x, axis=axis, keepdims=True)
    return (x - m) / jnp.sqrt(v + eps)

def _scatter_add(tgt, idx, src, axis=0):
    return tgt.at[idx].add(src)

def _segment_sum(src, seg, n):
    return jax.ops.segment_sum(src, seg, n)
kernel_name = 'mk_cond_seq_d2_seqx_r4_7f09a1'

def setup_inputs(seed: int=0):
    np.random.seed(seed)
    _w = jnp.asarray

    def _rec_inputs():
        import jax
        import jax.numpy as jnp
        _rk = jax.random.key(seed)
        x = 7.22e-05 + 1 * jax.random.normal(jax.random.fold_in(_rk, 1), (4, 512, 256), jnp.float32)
        _lenS = 512 - jax.random.randint(jax.random.fold_in(_rk, 7), (4,), 0, max(1, 512 // 4) + 1, jnp.int32)
        _lenS2 = 512 - jax.random.randint(jax.random.fold_in(_rk, 8), (4,), 0, max(1, 512 // 4) + 1, jnp.int32)
        cond_2048 = 0.00782532 + 1.00527 * jax.random.normal(jax.random.fold_in(_rk, 11), (4, 512), jnp.float32)
        _validS = jnp.arange(512)[None, :] < _lenS[:, None]
        _validS2 = jnp.arange(512)[None, :] < _lenS2[:, None]
        _causal = jnp.tril(jnp.ones((512, 512), dtype=bool))
        mask_BxS_ff1 = jnp.where(jnp.ones((4, 512), dtype=bool), 1.0, 0.0).astype(jnp.float32)
        return (x, cond_2048, mask_BxS_ff1)
    x, cond_2048, mask_BxS_ff1 = _rec_inputs()

    def _L0_cond_setup():
        import jax, jax.numpy as jnp
        import numpy as np
        B, S, C = (4, 512, 256)
        H = 16
        DH = C // H
        EPS = 1e-06

        def _rotate_half(t):
            d = t.shape[-1] // 2
            return jnp.concatenate([-t[..., d:], t[..., :d]], axis=-1)

        def _apply_rope(t, sin, cos):
            return t * cos + _rotate_half(t) * sin
        key = jax.random.key(seed)
        ks = jax.random.split(key, 6)
        x = jax.random.normal(ks[0], (B, S, C), dtype=jnp.float32)
        cond = jax.random.normal(ks[1], (B, 2 * C), dtype=jnp.float32)
        t = jnp.arange(S, dtype=jnp.float32)[:, None]
        inv_freq = 1.0 / 10000.0 ** (jnp.arange(DH, dtype=jnp.float32) / DH)
        ang = t * inv_freq[None, :]
        pos = jnp.stack([jnp.sin(ang), jnp.cos(ang)], axis=-1).reshape(S, 1, 2 * DH)
        rms_w = jnp.ones((C,), dtype=jnp.float32)
        w_cond = jax.random.normal(ks[2], (2 * C, 2 * C), dtype=jnp.float32) * (2 * C) ** (-0.5)
        w_qkv = jax.random.normal(ks[3], (C, 3 * C), dtype=jnp.float32) * C ** (-0.5)
        w_out = jax.random.normal(ks[4], (C, C), dtype=jnp.float32) * C ** (-0.5)
        return {'x': x, 'cond': cond, 'pos': pos, 'rms_w': rms_w, 'w_cond': w_cond, 'w_qkv': w_qkv, 'w_out': w_out}
    _L0_cond_all = _L0_cond_setup()
    _L0_cond_in = {k: v for k, v in _L0_cond_all.items() if k in ('pos', 'rms_w', 'w_cond', 'w_qkv', 'w_out')}
    del _L0_cond_all

    def _L1_cond_setup():
        import jax, jax.numpy as jnp
        import numpy as np
        B, T, D, H, TE = (8, 256, 256, 16, 512)
        LN_EPS = 1e-05

        def layer_norm(x, w, b):
            m = jnp.mean(x, axis=-1, keepdims=True)
            v = jnp.var(x, axis=-1, keepdims=True)
            return (x - m) / jnp.sqrt(v + LN_EPS) * w + b
        key = jax.random.key(seed)
        ks = jax.random.split(key, 8)
        s = lambda k, sh: jax.random.normal(k, sh, jnp.float32) * 0.02
        return dict(x=jax.random.normal(ks[0], (B, T, D), jnp.float32), emb=jax.random.normal(ks[1], (B, TE), jnp.float32), src_mask=jnp.ones((B, T), jnp.float32), norm_w=jnp.ones((D,), jnp.float32), norm_b=jnp.zeros((D,), jnp.float32), q_w=s(ks[2], (D, D)), q_b=jnp.zeros((D,), jnp.float32), k_w=s(ks[3], (D, D)), k_b=jnp.zeros((D,), jnp.float32), v_w=s(ks[4], (D, D)), v_b=jnp.zeros((D,), jnp.float32), emb_w=s(ks[5], (TE, 2 * D)), emb_b=jnp.zeros((2 * D,), jnp.float32), sb_norm_w=jnp.ones((D,), jnp.float32), sb_norm_b=jnp.zeros((D,), jnp.float32), out_w=s(ks[6], (D, D)), out_b=jnp.zeros((D,), jnp.float32))
    _L1_cond_all = _L1_cond_setup()
    _L1_cond_in = {k: v for k, v in _L1_cond_all.items() if k in ('norm_w', 'norm_b', 'q_w', 'q_b', 'k_w', 'k_b', 'v_w', 'v_b', 'emb_w', 'emb_b', 'sb_norm_w', 'sb_norm_b', 'out_w', 'out_b')}
    del _L1_cond_all
    return {'x': x, 'cond_2048': cond_2048, 'mask_BxS_ff1': mask_BxS_ff1, 'L0_cond_pos': _L0_cond_in['pos'], 'L0_cond_rms_w': _L0_cond_in['rms_w'], 'L0_cond_w_cond': _L0_cond_in['w_cond'], 'L0_cond_w_qkv': _L0_cond_in['w_qkv'], 'L0_cond_w_out': _L0_cond_in['w_out'], 'L1_cond_norm_w': _L1_cond_in['norm_w'], 'L1_cond_norm_b': _L1_cond_in['norm_b'], 'L1_cond_q_w': _L1_cond_in['q_w'], 'L1_cond_q_b': _L1_cond_in['q_b'], 'L1_cond_k_w': _L1_cond_in['k_w'], 'L1_cond_k_b': _L1_cond_in['k_b'], 'L1_cond_v_w': _L1_cond_in['v_w'], 'L1_cond_v_b': _L1_cond_in['v_b'], 'L1_cond_emb_w': _L1_cond_in['emb_w'], 'L1_cond_emb_b': _L1_cond_in['emb_b'], 'L1_cond_sb_norm_w': _L1_cond_in['sb_norm_w'], 'L1_cond_sb_norm_b': _L1_cond_in['sb_norm_b'], 'L1_cond_out_w': _L1_cond_in['out_w'], 'L1_cond_out_b': _L1_cond_in['out_b']}

def reference(x, cond_2048, mask_BxS_ff1, L0_cond_pos, L0_cond_rms_w, L0_cond_w_cond, L0_cond_w_qkv, L0_cond_w_out, L1_cond_norm_w, L1_cond_norm_b, L1_cond_q_w, L1_cond_q_b, L1_cond_k_w, L1_cond_k_b, L1_cond_v_w, L1_cond_v_b, L1_cond_emb_w, L1_cond_emb_b, L1_cond_sb_norm_w, L1_cond_sb_norm_b, L1_cond_out_w, L1_cond_out_b):
    import jax
    import jax.numpy as jnp

    def _L0_cond_ref(x, cond, pos, rms_w, w_cond, w_qkv, w_out):
        import jax, jax.numpy as jnp
        import numpy as np
        B, S, C = (4, 512, 256)
        H = 16
        DH = C // H
        EPS = 1e-06

        def _rotate_half(t):
            d = t.shape[-1] // 2
            return jnp.concatenate([-t[..., d:], t[..., :d]], axis=-1)

        def _apply_rope(t, sin, cos):
            return t * cos + _rotate_half(t) * sin
        b, s, c = x.shape
        residual = x
        xn = x * jax.lax.rsqrt(jnp.mean(x * x, axis=-1, keepdims=True) + EPS) * rms_w
        ss = cond @ w_cond
        scale, shift = (ss[:, :c], ss[:, c:])
        xm = xn * (1.0 + scale[:, None, :]) + shift[:, None, :]
        qkv = xm @ w_qkv
        q, k, v = jnp.split(qkv, 3, axis=-1)
        q = q.reshape(b, s, H, DH)
        k = k.reshape(b, s, H, DH)
        v = v.reshape(b, s, H, DH)
        sc = pos.reshape(s, 1, DH, 2)
        sin, cos = (sc[..., 0], sc[..., 1])
        q = _apply_rope(q, sin, cos)
        k = _apply_rope(k, sin, cos)
        scores = jnp.einsum('bqhd,bkhd->bhqk', q, k) * DH ** (-0.5)
        attn = jax.nn.softmax(scores, axis=-1)
        o = jnp.einsum('bhqk,bkhd->bqhd', attn, v).reshape(b, s, c)
        return o @ w_out + residual

    def _L1_cond_ref(x, emb, src_mask, norm_w, norm_b, q_w, q_b, k_w, k_b, v_w, v_b, emb_w, emb_b, sb_norm_w, sb_norm_b, out_w, out_b):
        import jax, jax.numpy as jnp
        import numpy as np
        B, T, D, H, TE = (8, 256, 256, 16, 512)
        LN_EPS = 1e-05

        def layer_norm(x, w, b):
            m = jnp.mean(x, axis=-1, keepdims=True)
            v = jnp.var(x, axis=-1, keepdims=True)
            return (x - m) / jnp.sqrt(v + LN_EPS) * w + b
        Bx, Tx, Dx = x.shape
        xn = layer_norm(x, norm_w, norm_b)
        q = (xn @ q_w + q_b).reshape(Bx, Tx, H, -1)
        k = (xn @ k_w + k_b).reshape(Bx, Tx, H, -1)
        att = jnp.einsum('bnhl,bmhl->bnmh', q, k)
        mask = src_mask.reshape(Bx, 1, Tx, 1)
        att = att + (1.0 - mask) * -1000000.0
        att = jax.nn.softmax(att, axis=2)
        v = ((xn @ v_w + v_b) * src_mask[:, :, None]).reshape(Bx, Tx, H, -1)
        y = jnp.einsum('bnmh,bmhl->bnhl', att, v).reshape(Bx, Tx, Dx)
        e = jax.nn.silu(emb) @ emb_w + emb_b
        scale, shift = jnp.split(e[:, None, :], 2, axis=2)
        h = layer_norm(y, sb_norm_w, sb_norm_b) * (1.0 + scale) + shift
        h = jax.nn.silu(h) @ out_w + out_b
        return x + h
    x = _L0_cond_ref(x, cond_2048, L0_cond_pos, L0_cond_rms_w, L0_cond_w_cond, L0_cond_w_qkv, L0_cond_w_out)
    x = _L1_cond_ref(x, cond_2048, mask_BxS_ff1, L1_cond_norm_w, L1_cond_norm_b, L1_cond_q_w, L1_cond_q_b, L1_cond_k_w, L1_cond_k_b, L1_cond_v_w, L1_cond_v_b, L1_cond_emb_w, L1_cond_emb_b, L1_cond_sb_norm_w, L1_cond_sb_norm_b, L1_cond_out_w, L1_cond_out_b)
    return x

_drawn_inputs = setup_inputs


def setup_inputs(seed=0):
    import zlib

    import numpy as np

    out = dict(_drawn_inputs(seed))
    spreads = {'L0_cond_rms_w': (1.0, 0.2),
     'L1_cond_norm_w': (1.0, 0.6),
     'L1_cond_norm_b': (0.0, 0.354),
     'L1_cond_q_b': (0.0, 0.8),
     'L1_cond_k_b': (0.0, 2.0),
     'L1_cond_v_b': (0.0, 0.1),
     'L1_cond_emb_b': (0.0, 0.422),
     'L1_cond_sb_norm_w': (1.0, 0.536),
     'L1_cond_sb_norm_b': (0.0, 0.597),
     'L1_cond_out_b': (0.0, 0.1)}
    factors = {'L1_cond_q_w': 8.0, 'L1_cond_k_w': 8.0}
    for name, (base, spread) in spreads.items():
        noise = np.random.default_rng([zlib.crc32(name.encode()), seed]).standard_normal(out[name].shape)
        drawn = base * np.exp(spread * noise) if base else spread * noise
        out[name] = jnp.asarray(drawn.astype(out[name].dtype))
    for name, factor in factors.items():
        out[name] = (out[name] * factor).astype(out[name].dtype)
    return out
```

```python
from contextlib import ExitStack

import concourse.bass as bass
from concourse import mybir

F32 = mybir.dt.float32
F16 = mybir.dt.float16
ALU = mybir.AluOpType
ACT = mybir.ActivationFunctionType
AX = mybir.AxisListType

P = 128
B, S, C, H = 4, 512, 256, 16
DH = C // H
TPB = S // P
NT = B * TPB
CT = C // P
COND = 2 * C
KC = COND // P
G = 4
NG = H // G
W32 = 32
QT = TPB
KT = TPB
EXPS = KT * G
MAXES = G * QT

HIGH_LOW = [(0, 0), (0, 1), (1, 0), (1, 1)]
ROW_MASK = 4 * DH
ROW_SHIFT = 96
MASK_UNIT = 64.0
MASK_VALUE = 1e6

RMS_W, NORM_W, NORM_B, Q_B, K_B, SBN_W, SBN_B, EMB_B, MASK = 0, 2, 4, 6, 8, 10, 12, 14, 18
VEC_ROWS = MASK + NT


class Buffers:
    pass


def build(nc, x, cond, mask, pos, rms_w, w_cond, w_qkv, w_out, norm_w, norm_b, q_w, q_b, k_w, k_b,
          v_w, v_b, emb_w, emb_b, sbn_w, sbn_b, out_w, out_b, out):
    m = Buffers()
    m.x, m.cond, m.mask, m.pos, m.out = x, cond, mask, pos, out
    m.rms_w, m.w_cond, m.w_qkv, m.w_out = rms_w, w_cond, w_qkv, w_out
    m.norm_w, m.norm_b, m.q_w, m.q_b, m.k_w, m.k_b, m.v_w, m.v_b = norm_w, norm_b, q_w, q_b, k_w, k_b, v_w, v_b
    m.emb_w, m.emb_b, m.sbn_w, m.sbn_b, m.out_w, m.out_b = emb_w, emb_b, sbn_w, sbn_b, out_w, out_b
    with ExitStack() as ctx:
        def sb(name, shape, dt=F32):
            return ctx.enter_context(nc.sbuf_tensor(name, shape, dt))

        m.bank = [ctx.enter_context(nc.psum_tensor(f"bank{i}", [P, 512], F32))[:, :] for i in range(8)]
        m.score_banks, m.max_banks, m.ACC, m.TURN = m.bank[0:2], m.bank[2:6], m.bank[6], m.bank[7]

        m.X = sb("X", [P, NT, C])
        m.V = sb("V", [P, NT, C])
        m.O = sb("O", [P, NT, C])
        m.XN = m.O
        m.xT = [sb(f"xT{i}", [P, CT, 512]) for i in range(2)]
        m.parts = [sb(f"parts{i}", [P, 2, 2 * CT, 512], F16) for i in range(2)]
        m.q_aug = [sb(f"q_aug{g}", [P, G, 512], F16) for g in range(NG)]
        m.k_aug = [sb(f"k_aug{g}", [P, G, 512], F16) for g in range(NG)]
        m.v_aug = [sb(f"v_aug{g}", [P, KT, G, W32]) for g in range(NG)]
        m.probs = [sb(f"probs{i}", [P, G, 512]) for i in range(KT)]
        m.oT = sb("oT", [P, 512])
        m.row_max = [sb(f"row_max{i}", [P, MAXES]) for i in range(2)]
        m.neg_max = [sb(f"neg_max{i}", [P, MAXES], F16) for i in range(2)]
        m.shift_rows = [sb(f"shift_rows{g}", [MAXES, P], F16) for g in range(NG)]
        m.inv_sum = sb("inv_sum", [P, QT, G, 1])

        m.wqkv = sb("wqkv", [P, CT, 3 * C])
        m.wo = sb("wo", [P, CT, C])
        m.wc = sb("wc", [P, KC, COND])
        m.wqkv1 = sb("wqkv1", [P, CT, 3 * C])
        m.wo1 = sb("wo1", [P, CT, C])
        m.vb_row = sb("vb_row", [P, C])
        m.ob_row = sb("ob_row", [P, C])
        m.ident = sb("ident", [P, P])
        m.ident16 = sb("ident16", [P, P], F16)
        m.vec_rows = sb("vec_rows", [VEC_ROWS, P])
        m.vec = sb("vec", [P, VEC_ROWS])
        m.cond_rows = sb("cond_rows", [B, COND])
        m.condT = sb("condT", [P, KC, B])
        m.ss_rows = sb("ss_rows", [B, COND])
        m.mod0_scale = sb("mod0_scale", [P, CT, B])
        m.mod0_shift = sb("mod0_shift", [P, CT, B])
        m.mod1 = sb("mod1", [P, KC, B])
        m.mod1_scale = sb("mod1_scale", [P, CT, B])
        m.mod1_shift = sb("mod1_shift", [P, CT, B])
        m.mask_row = sb("mask_row", [B, S])
        m.mask_hi = sb("mask_hi", [B, S], F16)
        m.mask_lo = sb("mask_lo", [B, S], F16)
        m.stats = sb("stats", [P, NT, 6])
        m.moments = sb("moments", [P, NT, 2])
        m.spread = sb("spread", [P, NT])
        m.rstd = sb("rstd", [P, NT])
        m.pos_rows = sb("pos_rows", [P, TPB, 2 * DH])
        m.pos_wide = [sb(f"pos_wide{i}", [P, P // DH, DH]) for i in range(2)]
        m.sinT = sb("sinT", [P, S])
        m.cosT = sb("cosT", [P, S])
        m.rotate = sb("rotate", [P, P])
        m.plain, m.with_cos = ([m.probs[0][:, 2 * j + i, :] for i in range(2)] for j in range(2))
        m.roped = [m.probs[1][:, i, :] for i in range(2)]
        m.aug_fill = sb("aug_fill", [P, 2])
        m.v_tmp = [sb(f"v_tmp{i}", [P, C]) for i in range(2)]
        m.y_out = [sb(f"y_out{i}", [P, C]) for i in range(2)]

        m.qk_dram = nc.dram_tensor("qk_parts", [B, 2, 2, C, S], F16, kind="Internal").ap()
        m.mask_dram = nc.dram_tensor("mask_parts", [2, B, S], F16, kind="Internal").ap()

        setup(nc, m)
        for layer in range(2):
            project(nc, layer, m)
            attend(nc, layer, m)
            finish(nc, layer, m)


def sems(ctx, nc, tag, *names):
    return [ctx.enter_context(nc.semaphore(f"{tag}_{n}")) for n in names]


def setup(nc, m):
    with ExitStack() as own:
        (small_in, wc_in, wl_in, ew_in, ident_made, const_made, vec_turned, vec_ready, cond_turned,
         cond_ready, ss_made, ss_copied, ss_turned, mod_step, mask_step, mask_out, emb_free, pos_wide_made,
         pos_turned, pos_copied, aug_made) = sems(
            own, nc, "set", "small_in", "wc_in", "wl_in", "ew_in", "ident_made", "const_made",
            "vec_turned", "vec_ready", "cond_turned", "cond_ready", "ss_made", "ss_copied", "ss_turned",
            "mod_step", "mask_step", "mask_out", "emb_free", "pos_wide_made", "pos_turned", "pos_copied", "aug_made")
        rows = [(RMS_W, m.rms_w), (NORM_W, m.norm_w), (NORM_B, m.norm_b), (Q_B, m.q_b), (K_B, m.k_b),
                (SBN_W, m.sbn_w), (SBN_B, m.sbn_b), (EMB_B, m.emb_b)]
        x_in = sems(own, nc, "set", *[f"x_in{b}" for b in range(B)])
        block = own.enter_context(nc.Block())

        @block.sync
        def _(sp):
            sp.dma_start(m.cond_rows[:, :], m.cond).then_inc(small_in, 16)
            for at, v in rows:
                n = v.shape[0] // P
                sp.dma_start(m.vec_rows[at:at + n, :], v.rearrange("(a p) -> a p", p=P)).then_inc(small_in, 16)
            sp.dma_start(m.vec_rows[MASK:MASK + NT, :], m.mask.rearrange("b (t p) -> (b t) p", p=P))\
                .then_inc(small_in, 16)
            sp.dma_start(m.mask_row[:, :], m.mask).then_inc(small_in, 16)
            sp.dma_start(m.pos_rows[:, :, :], m.pos.rearrange("(t p) o d -> p t (o d)", p=P)).then_inc(small_in, 16)
            for b in range(B):
                sp.dma_start(m.X[:, b * TPB:(b + 1) * TPB, :], m.x[b].rearrange("(t p) c -> p t c", p=P))\
                    .then_inc(x_in[b], 16)
            sp.wait_ge(emb_free, 1)
            sp.dma_start(m.wc[:, :, :], m.emb_w.rearrange("(k p) n -> p k n", p=P)).then_inc(ew_in, 16)
            sp.wait_ge(mask_step, 3)
            sp.dma_start(m.mask_dram[0], m.mask_hi[:, :]).then_inc(mask_out, 16)
            sp.dma_start(m.mask_dram[1], m.mask_lo[:, :]).then_inc(mask_out, 16)
            sp.wait_ge(mask_out, 32)
            for b in range(B):
                sp.wait_ge(x_in[b], 16)

        @block.scalar
        def _(act):
            act.dma_start(m.wc[:, :, :], m.w_cond.rearrange("(k p) n -> p k n", p=P)).then_inc(wc_in, 16)
            act.dma_start(m.wqkv[:, :, :], m.w_qkv.rearrange("(k p) n -> p k n", p=P)).then_inc(wl_in, 16)
            act.dma_start(m.wo[:, :, :], m.w_out.rearrange("(k p) n -> p k n", p=P)).then_inc(wl_in, 16)
            for i, w in enumerate((m.q_w, m.k_w, m.v_w)):
                act.dma_start(m.wqkv1[:, :, i * C:(i + 1) * C], w.rearrange("(k p) n -> p k n", p=P))\
                    .then_inc(wl_in, 16)
            act.dma_start(m.wo1[:, :, :], m.out_w.rearrange("(k p) n -> p k n", p=P)).then_inc(wl_in, 16)
            act.dma_start(m.vb_row[:, :], m.v_b.partition_broadcast(P)).then_inc(wl_in, 16)
            act.dma_start(m.ob_row[:, :], m.out_b.partition_broadcast(P)).then_inc(wl_in, 16)
            act.wait_ge(cond_turned, 2)
            act.wait_ge(ss_made, 1)
            act.activation(m.condT[:, :, :], m.TURN[:, 0:KC * B].rearrange("p (k b) -> p k b", b=B), ACT.Silu)\
                .then_inc(cond_ready, 1)
            act.wait_ge(wl_in, 16 * 8)

        @block.gpsimd
        def _(pool):
            for n, (t, v) in enumerate([(m.ident, 0.0), (m.ident16, 0.0)]):
                pool.memset(t[:, :], v).then_inc(ident_made, 1)
            pool.wait_ge(ident_made, 2)
            for t in (m.ident, m.ident16):
                pool.affine_select(out=t[:, :], in_=t[:, :], compare_op=ALU.not_equal, fill=1.0, base=0,
                                   pattern=[[-1, P]], channel_multiplier=1).then_inc(ident_made, 1)
            pool.memset(m.rotate[:, :], 0.0).then_inc(ident_made, 1)
            pool.wait_ge(ident_made, 5)
            halves = m.rotate[:, :].rearrange("p (h two d) -> p h two d", two=2, d=DH // 2)
            for half, (base, value) in enumerate([(-DH // 2, -1.0), (0, 1.0)]):
                pool.affine_select(out=halves[:, :, half, :], in_=halves[:, :, half, :], compare_op=ALU.not_equal,
                                   fill=value, base=base, pattern=[[-DH, P // DH], [-1, DH // 2]],
                                   channel_multiplier=1).then_inc(ident_made, 1)
            pool.memset(m.aug_fill[:, :], 0.0).then_inc(const_made, 1)
            pool.memset(m.probs[0][:, 0:2, :], 0.0).then_inc(const_made, 1)
            rows_of = [(0, ROW_MASK, MASK_UNIT), (0, ROW_MASK + 1, MASK_UNIT), (1, ROW_SHIFT, 1.0)]
            for n, (col, row, value) in enumerate(rows_of):
                pool.wait_ge(const_made, 2 + n)
                at = m.aug_fill[:, col:col + 1]
                pool.affine_select(out=at, in_=at, compare_op=ALU.not_equal, fill=value, base=-row,
                                   pattern=[[0, 1]], channel_multiplier=1).then_inc(const_made, 1)
            n = 2 + len(rows_of)
            for g in range(NG):
                pool.memset(m.v_aug[g][:, :, :, DH:W32], 0.0).then_inc(const_made, 1)
            pool.wait_ge(const_made, n + NG)
            for g in range(NG):
                pool.memset(m.v_aug[g][:, :, :, DH:DH + 1], 1.0).then_inc(const_made, 1)
            n += 2 * NG
            pool.wait_ge(wl_in, 16 * 8)
            pool.tensor_scalar(m.wqkv[:, :, 0:C], m.wqkv[:, :, 0:C], float(DH) ** -0.5, None, ALU.mult)\
                .then_inc(const_made, 1)
            pool.wait_ge(const_made, n + 1)

        @block.tensor
        def _(pe):
            pe.wait_ge(ident_made, 4)
            pe.wait_ge(small_in, 16 * (len(rows) + 4))
            nc.tensor.transpose(m.bank[0][:, 0:VEC_ROWS], m.vec_rows[:, :], m.ident[0:VEC_ROWS, 0:VEC_ROWS])\
                .then_inc(vec_turned, 1)
            for layer in range(2):
                if layer:
                    for t in range(TPB):
                        pe.wait_ge(pos_wide_made, 2 * (t + 1))
                        for i in range(2):
                            last = nc.tensor.transpose(m.bank[4 + i][:, t * P:(t + 1) * P],
                                                       m.pos_wide[i][:, :, :].rearrange("p h d -> p (h d)"),
                                                       m.ident[:, :])
                        last.then_inc(pos_turned, 1)
                    pe.wait_ge(cond_ready, 1)
                for k in range(KC):
                    last = nc.tensor.transpose(m.TURN[:, k * B:(k + 1) * B], m.cond_rows[:, k * P:(k + 1) * P],
                                               m.ident[0:B, 0:B])
                last.then_inc(cond_turned, 1)
                pe.wait_ge(cond_ready, 1 + layer)
                pe.wait_ge(ew_in if layer else wc_in, 16)
                if layer:
                    pe.wait_ge(ss_copied, 1)
                for k in range(KC):
                    last = nc.tensor.matmul(m.ACC[0:B, :], m.condT[:, k, :], m.wc[:, k, :],
                                            start=(k == 0), stop=(k == KC - 1))
                last.then_inc(ss_made, 1)
                pe.wait_ge(ss_copied, 1 + layer)
                for k in range(KC):
                    last = nc.tensor.transpose(m.bank[1 + layer][:, k * B:(k + 1) * B],
                                               m.ss_rows[:, k * P:(k + 1) * P], m.ident[0:B, 0:B])
                last.then_inc(ss_turned, 1)

        @block.vector
        def _(dve):
            dve.wait_ge(vec_turned, 1)
            dve.tensor_copy(m.vec[:, :], m.bank[0][:, 0:VEC_ROWS]).then_inc(vec_ready, 1)
            dve.wait_ge(const_made, 2 + 3)
            zeros = m.probs[0][:, 0:2, :].bitcast(F16).rearrange("p a (b n) -> p (a b) n", b=2)
            for g in range(NG):
                for i, aug in enumerate((m.q_aug, m.k_aug)):
                    dve.tensor_scalar(aug[g][:, :, :], zeros, m.aug_fill[:, i:i + 1], None, ALU.add)\
                       .then_inc(aug_made, 1)
            dve.wait_ge(aug_made, 2 * NG)
            dve.wait_ge(small_in, 16 * (len(rows) + 4))
            dve.tensor_scalar(m.mask_row[:, :], m.mask_row[:, :], -1.0, MASK_VALUE / MASK_UNIT, ALU.add, ALU.mult)\
                .then_inc(mask_step, 1)
            dve.wait_ge(mask_step, 1)
            dve.tensor_copy(m.mask_hi[:, :], m.mask_row[:, :]).then_inc(mask_step, 1)
            dve.wait_ge(mask_step, 2)
            dve.tensor_tensor(m.mask_lo[:, :], m.mask_row[:, :], m.mask_hi[:, :], ALU.subtract).then_inc(mask_step, 1)
            dve.wait_ge(cond_turned, 1)
            dve.tensor_copy(m.condT[:, :, :], m.TURN[:, 0:KC * B].rearrange("p (k b) -> p k b", b=B))\
                .then_inc(cond_ready, 1)
            dve.wait_ge(ss_made, 1)
            dve.tensor_copy(m.ss_rows[:, :], m.ACC[0:B, :]).then_inc(ss_copied, 1)
            dve.wait_ge(ss_copied, 1)
            dve.tensor_copy(spare_cell(m), m.vec[:, 0:1]).then_inc(emb_free, 1)
            dve.wait_ge(ss_turned, 1)
            dve.wait_ge(vec_ready, 1)
            ss = m.bank[1][:, 0:KC * B].rearrange("p (k b) -> p k b", b=B)
            for h in range(CT):
                dve.tensor_scalar(m.mod0_scale[:, h, :], ss[:, h, :], 1.0, m.vec[:, RMS_W + h:RMS_W + h + 1],
                                  ALU.add, ALU.mult).then_inc(mod_step, 1)
            dve.tensor_copy(m.mod0_shift[:, :, :], ss[:, CT:2 * CT, :]).then_inc(mod_step, 1)
            for t in range(TPB):
                if t:
                    dve.wait_ge(pos_turned, t)
                for i in range(2):
                    both = m.pos_rows[:, t, :].rearrange("p (d two) -> p two d", two=2)
                    dve.tensor_copy(m.pos_wide[i][:, :, :], both[:, i:i + 1, :].broadcast_to([P, P // DH, DH]))\
                       .then_inc(pos_wide_made, 1)
            for t in range(NT):
                if t % TPB == 0:
                    dve.wait_ge(x_in[t // TPB], 16)
                dve.bn_stats(m.stats[:, t, :], m.X[:, t, :]).then_inc(mod_step, 1)
            dve.wait_ge(mod_step, 3 + NT)
            for t in range(NT):
                dve.bn_aggr(m.moments[:, t, :], m.stats[:, t, :]).then_inc(mod_step, 1)
            done = 3 + 2 * NT
            dve.wait_ge(ss_made, 2)
            dve.tensor_copy(m.ss_rows[:, :], m.ACC[0:B, :]).then_inc(ss_copied, 1)
            dve.wait_ge(ss_turned, 2)
            es = m.bank[2][:, 0:KC * B].rearrange("p (k b) -> p k b", b=B)
            for k in range(KC):
                dve.tensor_scalar(m.mod1[:, k, :], es[:, k, :], m.vec[:, EMB_B + k:EMB_B + k + 1],
                                  1.0 if k < CT else 0.0, ALU.add, ALU.add).then_inc(mod_step, 1)
            dve.wait_ge(mod_step, done + KC)
            for h in range(CT):
                dve.tensor_scalar(m.mod1_scale[:, h, :], m.mod1[:, h, :], m.vec[:, SBN_W + h:SBN_W + h + 1], None,
                                  ALU.mult).then_inc(mod_step, 1)
                dve.scalar_tensor_tensor(m.mod1_shift[:, h, :], m.mod1[:, h, :],
                                         m.vec[:, SBN_B + h:SBN_B + h + 1], m.mod1[:, CT + h, :],
                                         ALU.mult, ALU.add).then_inc(mod_step, 1)
            dve.wait_ge(pos_turned, TPB)
            dve.tensor_copy(m.sinT[:, :], m.bank[4]).then_inc(pos_copied, 1)
            dve.tensor_copy(m.cosT[:, :], m.bank[5]).then_inc(pos_copied, 1)
            dve.wait_ge(pos_copied, 2)
            dve.wait_ge(mod_step, done + KC + 2 * CT)


def spare_cell(m):
    return m.spread[:, 0:1]


def normalise(dve, act, m, step, root, centred):
    if dve is not None:
        if centred:
            dve.tensor_scalar(m.spread[:, :], m.moments[:, :, 1], 1e-5, None, ALU.add).then_inc(step, 1)
        else:
            dve.tensor_tensor(m.rstd[:, :], m.moments[:, :, 0], m.moments[:, :, 0], ALU.mult).then_inc(step, 1)
            dve.wait_ge(step, 1)
            dve.scalar_tensor_tensor(m.spread[:, :], m.moments[:, :, 1], 1e-6, m.rstd[:, :],
                                     ALU.add, ALU.add).then_inc(step, 1)
        n = 1 if centred else 2
        dve.wait_ge(root, 1)
        dve.reciprocal(m.rstd[:, :], m.spread[:, :]).then_inc(step, 1)
        n += 1
        dve.wait_ge(step, n)
    if act is not None:
        act.wait_ge(step, 1 if centred else 2)
        act.activation(m.spread[:, :], m.spread[:, :], ACT.Sqrt).then_inc(root, 1)


def normal_tile(dve, m, src, t, centred):
    if centred:
        return dve.tensor_scalar(m.XN[:, t, :], src[:, t, :], m.moments[:, t, 0:1], m.rstd[:, t:t + 1],
                                 ALU.subtract, ALU.mult)
    return dve.tensor_scalar(m.XN[:, t, :], src[:, t, :], m.rstd[:, t:t + 1], None, ALU.mult)


def project(nc, layer, m):
    w = m.wqkv1 if layer else m.wqkv
    with ExitStack() as own:
        (step, root, xn_ready, x_turned, xT_ready, qk_made, plain_ready, rotated, sin_done, cos_done, rope_done,
         high_made, low_made, v_made, v_read, v_ready) = sems(
            own, nc, f"pr{layer}", "step", "root", "xn_ready", "x_turned", "xT_ready", "qk_made", "plain_ready",
            "rotated", "sin_done", "cos_done", "rope_done", "high_made", "low_made", "v_made", "v_read",
            "v_ready")
        parts_out = sems(own, nc, f"pr{layer}", *[f"parts_out{i}" for i in range(4 * CT)])
        block = own.enter_context(nc.Block())
        NQ = 2 * CT
        QK_BANKS, V_BANKS, ROT_BANKS = (2, 3), (4, 5), (6, 7)

        def part(n, hl):
            return m.parts[n // NQ % 2][:, hl, n % NQ, :]

        def bias(n):
            at = (Q_B if n % NQ < CT else K_B) + n % CT
            return m.vec[:, at:at + 1]

        def parts_free(engine, n):
            if n >= 2 * NQ:
                engine.wait_ge(parts_out[n % (2 * NQ)], 16 * (n // (2 * NQ)))

        @block.vector
        def _(dve):
            normalise(dve, None, m, step, root, bool(layer))
            for t in range(NT):
                normal_tile(dve, m, m.X, t, bool(layer)).then_inc(xn_ready, 1)

            def rope(n):
                f = m.roped[n % 2][:, :]
                dve.wait_ge(rotated, n + 1)
                if n >= 2:
                    dve.wait_ge(high_made, n - 1)
                    dve.wait_ge(low_made, n - 1)
                dve.tensor_tensor(f, m.bank[ROT_BANKS[n % 2]], m.sinT[:, :], ALU.mult).then_inc(sin_done, 1)
                dve.wait_ge(sin_done, n + 1)
                dve.wait_ge(cos_done, n + 1)
                dve.tensor_tensor(f, f, m.with_cos[n % 2][:, :], ALU.add).then_inc(rope_done, 1)

            def low(n):
                dve.wait_ge(high_made, n + 1)
                parts_free(dve, n)
                if layer:
                    ins = dve.scalar_tensor_tensor(part(n, 1), m.bank[QK_BANKS[n % 2]], bias(n), part(n, 0),
                                                   ALU.add, ALU.subtract)
                else:
                    ins = dve.tensor_tensor(part(n, 1), m.roped[n % 2][:, :], part(n, 0), ALU.subtract)
                ins.then_inc(low_made, 1)

            def v_bias(n):
                dve.wait_ge(v_made, n + 1)
                if n >= 2:
                    dve.wait_ge(v_ready, n - 1)
                dve.tensor_tensor(m.v_tmp[n % 2][:, :], m.bank[V_BANKS[n % 2]][:, 0:C], m.vb_row[:, :],
                                  ALU.add).then_inc(v_read, 1)

            for n in range(NQ * B):
                if layer:
                    low(n)
                    if n % NQ == NQ - 1:
                        for t in range(TPB):
                            v_bias(n // NQ * TPB + t)
                else:
                    rope(n)
                    if n:
                        low(n - 1)
            if not layer:
                low(NQ * B - 1)

        @block.scalar
        def _(act):
            normalise(None, act, m, step, root, bool(layer))

            def turn(b):
                for h in range(CT):
                    act.wait_ge(x_turned, CT * b + h + 1)
                    if b >= 2:
                        act.wait_ge(v_made, TPB * (b - 1))
                    if layer:
                        scale, shift = m.vec[:, NORM_W + h:NORM_W + h + 1], m.vec[:, NORM_B + h:NORM_B + h + 1]
                    else:
                        scale, shift = m.mod0_scale[:, h, b:b + 1], m.mod0_shift[:, h, b:b + 1]
                    act.activation(m.xT[b % 2][:, h, :], m.bank[h], ACT.Identity, bias=shift, scale=scale)\
                        .then_inc(xT_ready, 1)

            def plain(n):
                act.wait_ge(qk_made, n + 1)
                if n >= 2:
                    act.wait_ge(rotated, n - 1)
                    act.wait_ge(cos_done, n - 1)
                act.activation(m.plain[n % 2][:, :], m.bank[QK_BANKS[n % 2]], ACT.Copy).then_inc(plain_ready, 1)

            def high(n):
                parts_free(act, n)
                if layer:
                    act.wait_ge(qk_made, n + 1)
                    ins = act.activation(part(n, 0), m.bank[QK_BANKS[n % 2]], ACT.Identity, bias=bias(n))
                else:
                    act.wait_ge(rope_done, n + 1)
                    ins = act.activation(part(n, 0), m.roped[n % 2][:, :], ACT.Copy)
                ins.then_inc(high_made, 1)

            turn(0)
            for n in range(NQ * B):
                b = n // NQ
                if layer:
                    high(n)
                else:
                    plain(n)
                    if n:
                        high(n - 1)
                if n % NQ == NQ - 1:
                    if b + 1 < B:
                        turn(b + 1)
                    if not layer:
                        for t in range(TPB * b, TPB * (b + 1)):
                            act.wait_ge(v_made, t + 1)
                            act.activation(m.V[:, t, :], m.bank[V_BANKS[t % 2]][:, 0:C], ACT.Copy).then_inc(v_read, 1)
            if not layer:
                high(NQ * B - 1)

        @block.gpsimd
        def _(pool):
            if layer:
                for n in range(NT):
                    pool.wait_ge(v_read, n + 1)
                    pool.tensor_scalar(m.V[:, n, :], m.v_tmp[n % 2][:, :], m.vec[:, MASK + n:MASK + n + 1], None,
                                       ALU.mult).then_inc(v_ready, 1)
            else:
                for n in range(NQ * B):
                    pool.wait_ge(plain_ready, n + 1)
                    if n >= 2:
                        pool.wait_ge(rope_done, n - 1)
                    pool.tensor_tensor(m.with_cos[n % 2][:, :], m.plain[n % 2][:, :], m.cosT[:, :], ALU.mult)\
                        .then_inc(cos_done, 1)

        @block.tensor
        def _(pe):
            def turn(b):
                for h in range(CT):
                    if b:
                        pe.wait_ge(xT_ready, CT * (b - 1) + h + 1)
                    for t in range(TPB):
                        pe.wait_ge(xn_ready, TPB * b + t + 1)
                        last = nc.tensor.transpose(m.bank[h][:, t * P:(t + 1) * P],
                                                   m.XN[:, TPB * b + t, h * P:(h + 1) * P], m.ident[:, :])
                    last.then_inc(x_turned, 1)

            def queries_keys(n):
                if n >= 2:
                    pe.wait_ge(low_made if layer else plain_ready, n - 1)
                i = n % NQ
                for k in range(CT):
                    last = nc.tensor.matmul(m.bank[QK_BANKS[n % 2]], w[:, k, i * P:(i + 1) * P],
                                            m.xT[n // NQ % 2][:, k, :], start=(k == 0), stop=(k == CT - 1))
                last.then_inc(qk_made, 1)

            def rotate(n):
                pe.wait_ge(plain_ready, n + 1)
                if n >= 2:
                    pe.wait_ge(sin_done, n - 1)
                nc.tensor.matmul(m.bank[ROT_BANKS[n % 2]], m.rotate[:, :], m.plain[n % 2][:, :],
                                 start=True, stop=True).then_inc(rotated, 1)

            turn(0)
            for b in range(B):
                pe.wait_ge(xT_ready, CT * (b + 1))
                for n in range(NQ * b, NQ * (b + 1)):
                    queries_keys(n)
                    if n and not layer:
                        rotate(n - 1)
                if b + 1 < B:
                    turn(b + 1)
                for t in range(TPB):
                    n = TPB * b + t
                    if n >= 2:
                        pe.wait_ge(v_read, n - 1)
                    for k in range(CT):
                        last = nc.tensor.matmul(m.bank[V_BANKS[n % 2]][:, 0:C], m.xT[b % 2][:, k, t * P:(t + 1) * P],
                                                w[:, k, 2 * C:3 * C], start=(k == 0), stop=(k == CT - 1))
                    last.then_inc(v_made, 1)
            if not layer:
                rotate(NQ * B - 1)

        @block.sync
        def _(sp):
            for n in range(NQ * B):
                b, i = divmod(n, NQ)
                sp.wait_ge(low_made, n + 1)
                sp.dma_start(m.qk_dram[b, i // CT, :, (i % CT) * P:(i % CT + 1) * P, :]
                             .rearrange("l p t -> p l t"), m.parts[b % 2][:, :, i, :])\
                    .then_inc(parts_out[n % (2 * NQ)], 16)
            for out in parts_out:
                sp.wait_ge(out, 16 * B // 2)


def attend(nc, layer, m):
    LOADS = 8 + 2 * layer
    LEAD = 2
    with ExitStack() as own:
        (row_scores_made, max_made, shift_made, shift_turned, shift_copied,
         scores_made, exp_made, v_in, probs_used, acc_copied, o_turned, o_written, inv_made) = sems(
            own, nc, f"at{layer}", "row_scores_made", "max_made", "shift_made", "shift_turned",
            "shift_copied", "scores_made", "exp_made", "v_in", "probs_used", "acc_copied",
            "o_turned", "o_written", "inv_made")
        operands_in = sems(own, nc, f"at{layer}", *[f"operands_in{g}" for g in range(NG)])
        shift_in = sems(own, nc, f"at{layer}", *[f"shift_in{g}" for g in range(NG)])
        block = own.enter_context(nc.Block())
        turn16 = m.TURN.bitcast(F16)

        def after(b, g, groups):
            return b + (g + groups) // NG, (g + groups) % NG

        def batches(engine, body):
            with engine.Fori(0, B - 1) as b:
                body(b, False)
            body(B - 1, True)

        @block.sync
        def _(sp):
            def load(b, g):
                for r, (qp, kp) in enumerate(HIGH_LOW):
                    for aug, side, part in ((m.q_aug, 0, qp), (m.k_aug, 1, kp)):
                        sp.dma_start(aug[g][r * DH:(r + 1) * DH, :, :],
                                     m.qk_dram[b, side, part, g * G * DH:(g + 1) * G * DH, :]
                                     .rearrange("(h d) t -> d h t", d=DH)).then_inc(operands_in[g], 16)
                if layer:
                    for part in range(2):
                        row = ROW_MASK + part
                        sp.dma_start(m.k_aug[g][row:row + 1, :, :],
                                     m.mask_dram[part, bass.ds(b, 1), :].unsqueeze(1).broadcast_to([1, G, S]))\
                            .then_inc(operands_in[g], 16)

            def shift(b, g):
                sp.wait_ge(shift_copied, b * NG + g + 1)
                sp.dma_start(m.q_aug[g][ROW_SHIFT:ROW_SHIFT + 1, :, :], m.shift_rows[g][:, :])\
                    .then_inc(shift_in[g], 16)

            for g in range(NG):
                load(0, g)
            shift(0, 0)

            def body(b, last):
                for g in range(NG):
                    s = b * NG + g
                    if not (last and g == NG - 1):
                        shift(*after(b, g, 1))
                    if not last:
                        sp.wait_ge(scores_made, EXPS * (s + 1))
                        load(b + 1, g)

            batches(sp, body)

        @block.gpsimd
        def _(pool):
            def values(b, g):
                pool.tensor_copy(m.v_aug[g][:, :, :, 0:DH],
                                 m.V[:, bass.ds(b * TPB, TPB), g * G * DH:(g + 1) * G * DH]
                                 .rearrange("p t (h d) -> p t h d", d=DH)).then_inc(v_in, 1)

            for g in range(NG):
                values(0, g)

            def body(b, last):
                if last:
                    return
                for g in range(NG):
                    s = b * NG + g
                    pool.wait_ge(probs_used, KT + KT * (s + 1))
                    values(b + 1, g)

            batches(pool, body)

        @block.tensor
        def _(pe):
            def row_scores(b, g, j):
                h, q = divmod(j, QT)
                if j == 0:
                    pe.wait_ge(operands_in[g], 16 * LOADS * (b + 1))
                n = MAXES * (b * NG + g) + j
                if not (isinstance(n, int) and n < 4):
                    pe.wait_ge(max_made, n - 3)
                nc.tensor.matmul(m.max_banks[j % 4], m.q_aug[g][0:ROW_SHIFT, h, q * P:(q + 1) * P],
                                 m.k_aug[g][0:ROW_SHIFT, h, :], start=True, stop=True)\
                    .then_inc(row_scores_made, 1)

            def turn_shift(s, g, turned):
                pe.wait_ge(shift_made, s + 1)
                pe.wait_ge(o_written, 1 + turned)
                nc.tensor.transpose(turn16[0:MAXES, 0:P], m.neg_max[g % 2][:, :], m.ident16[:, :])\
                    .then_inc(shift_turned, 1)

            def scores(b, g, k, h):
                if k == 0 and h == 0:
                    pe.wait_ge(shift_in[g], 16 * (b + 1))
                pe.wait_ge(exp_made, EXPS * (b * NG + g) + G * k + h + 1)
                nc.tensor.matmul(m.score_banks[h % 2], m.k_aug[g][0:ROW_SHIFT + 1, h, k * P:(k + 1) * P],
                                 m.q_aug[g][0:ROW_SHIFT + 1, h, :], start=True, stop=True)\
                    .then_inc(scores_made, 1)

            def values(s, g, k, half):
                if k == 0 and half == 0:
                    pe.wait_ge(v_in, s + 1)
                    pe.wait_ge(acc_copied, 1 + s)
                pe.wait_ge(exp_made, 2 + EXPS * s + G * (k + 1))
                at = slice(half * S // 2, (half + 1) * S // 2)
                for h in range(G):
                    last = nc.tensor.matmul(m.ACC[W32 * h:W32 * (h + 1), at], m.v_aug[g][:, k, h, :],
                                            m.probs[k][:, h, at], start=(k == 0 and half == 0), stop=(k == KT - 1),
                                            tile_position=(0, W32 * h), skip_group_check=True)
                if half == 1:
                    last.then_inc(probs_used, 1)

            def turn_output(s, shifts):
                pe.wait_ge(acc_copied, 1 + s + 1)
                pe.wait_ge(shift_copied, shifts)
                pe.wait_ge(o_written, 1 + s)
                for q in range(QT):
                    last = nc.tensor.transpose(m.TURN[:, q * P:(q + 1) * P], m.oT[:, q * P:(q + 1) * P],
                                               m.ident[:, :])
                last.then_inc(o_turned, 1)

            for s in range(LEAD):
                for j in range(MAXES):
                    row_scores(0, s, j)
                if s == 0:
                    turn_shift(0, 0, 0)

            def body(b, last):
                for g in range(NG):
                    s = b * NG + g
                    ahead = not (last and g >= NG - LEAD)
                    final = last and g == NG - 1
                    for k in range(KT):
                        for h in range(G):
                            scores(b, g, k, h)
                            if ahead:
                                row_scores(*after(b, g, LEAD), G * k + h)
                            if h % 2 and k > 0:
                                values(s, g, k - 1, h // 2)
                            if h % 2 and k == 0 and g > 0:
                                values(s - 1, g - 1, KT - 1, h // 2)
                        if k == 1 and not final:
                            turn_shift(s + 1, (g + 1) % NG, s if g == 0 else s - 1)
                        if k == 2 and g > 0:
                            turn_output(s - 1, s + 2 - (1 if final else 0))
                for half in range(2):
                    values(b * NG + NG - 1, NG - 1, KT - 1, half)
                turn_output(b * NG + NG - 1, b * NG + NG + (0 if last else 1))

            batches(pe, body)

        @block.scalar
        def _(act):
            act.sem_inc(exp_made, 2)
            act.sem_inc(probs_used, KT)
            act.sem_inc(acc_copied, 1)
            act.sem_inc(o_turned, 1)
            act.sem_inc(o_written, 1)

            def copy_shift(b, g):
                act.wait_ge(shift_turned, b * NG + g + 1)
                act.activation(m.shift_rows[g][:, :], turn16[0:MAXES, 0:P], ACT.Copy).then_inc(shift_copied, 1)

            def copy_output(s):
                act.wait_ge(probs_used, KT + KT * (s + 1))
                act.wait_ge(o_turned, 1 + s)
                act.activation(m.oT[:, :], m.ACC, ACT.Copy).then_inc(acc_copied, 1)

            copy_shift(0, 0)

            def body(b, last):
                for g in range(NG):
                    s = b * NG + g
                    for k in range(KT):
                        for h in range(G):
                            act.wait_ge(scores_made, EXPS * s + G * k + h + 1)
                            if h == 0:
                                act.wait_ge(probs_used, KT * s + k + 1)
                            act.activation(m.probs[k][:, h, :], m.score_banks[h % 2], ACT.Exp)\
                                .then_inc(exp_made, 1)
                        if k == 0 and g > 0:
                            copy_output(s - 1)
                        if k == 1 and not (last and g == NG - 1):
                            copy_shift(*after(b, g, 1))
                copy_output(b * NG + NG - 1)

            batches(act, body)

        @block.vector
        def _(dve):
            def maximum(s, g, j):
                dve.wait_ge(row_scores_made, MAXES * s + j + 1)
                if j == 0 and not (isinstance(s, int) and s < 2):
                    dve.wait_ge(shift_made, s - 1)
                dve.tensor_reduce(m.row_max[g % 2][:, j:j + 1], m.max_banks[j % 4], AX.X, ALU.max)\
                    .then_inc(max_made, 1)

            def negate(s, g):
                dve.wait_ge(max_made, MAXES * (s + 1))
                if not (isinstance(s, int) and s < 2):
                    dve.wait_ge(shift_turned, s - 1)
                dve.tensor_scalar(m.neg_max[g % 2][:, :], m.row_max[g % 2][:, :], -1.0, None, ALU.mult)\
                    .then_inc(shift_made, 1)

            def write_output(b, g):
                s = b * NG + g
                turned = m.TURN.rearrange("p (q h w) -> p q h w", q=QT, h=G)
                dve.wait_ge(o_turned, 1 + s + 1)
                dve.wait_ge(o_written, 1 + s)
                dve.reciprocal(m.inv_sum[:, :, :, :], turned[:, :, :, DH:DH + 1]).then_inc(inv_made, 1)
                dve.wait_ge(inv_made, s + 1)
                dve.tensor_tensor(m.O[:, bass.ds(b * TPB, TPB), g * G * DH:(g + 1) * G * DH]
                                  .rearrange("p t (h d) -> p t h d", d=DH),
                                  turned[:, :, :, 0:DH], m.inv_sum[:, :, :, :].broadcast_to([P, QT, G, DH]),
                                  ALU.mult).then_inc(o_written, 1)

            for s in range(LEAD):
                for j in range(MAXES):
                    maximum(s, s, j)
                negate(s, s)

            def body(b, last):
                for g in range(NG):
                    s = b * NG + g
                    ahead = not (last and g >= NG - LEAD)
                    for j in range(MAXES):
                        if ahead:
                            maximum(s + LEAD, (g + LEAD) % NG, j)
                        if j == 3 * QT + 1 and g > 0:
                            write_output(b, g - 1)
                    if ahead:
                        negate(s + LEAD, (g + LEAD) % NG)
                write_output(b, NG - 1)

            batches(dve, body)


def finish(nc, layer, m):
    w = m.wo1 if layer else m.wo
    with ExitStack() as own:
        (step, root, src_ready, turned, srcT_ready, y_made, y_added, stat_step, xb_added) = sems(
            own, nc, f"fi{layer}", "step", "root", "src_ready", "turned", "srcT_ready", "y_made", "y_added",
            "stat_step", "xb_added")
        y_out_done = sems(own, nc, f"fi{layer}", "y_out_done0", "y_out_done1")
        block = own.enter_context(nc.Block())
        src = m.XN if layer else m.O

        @block.gpsimd
        def _(pool):
            if layer:
                pool.tensor_tensor(m.X[:, :, :], m.X[:, :, :],
                                   m.ob_row[:, :].unsqueeze(1).broadcast_to([P, NT, C]), ALU.add)\
                    .then_inc(xb_added, 1)

        @block.vector
        def _(dve):
            if layer:
                for t in range(NT):
                    dve.bn_stats(m.stats[:, t, :], m.O[:, t, :]).then_inc(stat_step, 1)
                dve.wait_ge(stat_step, NT)
                for t in range(NT):
                    dve.bn_aggr(m.moments[:, t, :], m.stats[:, t, :]).then_inc(stat_step, 1)
                dve.wait_ge(stat_step, 2 * NT)
                normalise(dve, None, m, step, root, True)
                for t in range(NT):
                    normal_tile(dve, m, m.O, t, True).then_inc(src_ready, 1)
                dve.wait_ge(xb_added, 1)
            for t in range(NT):
                dve.wait_ge(y_made, t + 1)
                if layer:
                    if t >= 2:
                        dve.wait_ge(y_out_done[t % 2], 16 * (t // 2))
                    dst = m.y_out[t % 2][:, :]
                else:
                    dst = m.X[:, t, :]
                dve.tensor_tensor(dst, m.bank[2 + t % 2][:, 0:C], m.X[:, t, :], ALU.add).then_inc(y_added, 1)
                if not layer:
                    dve.wait_ge(y_added, t + 1)
                    dve.bn_stats(m.stats[:, t, :], m.X[:, t, :]).then_inc(stat_step, 1)
            if not layer:
                dve.wait_ge(stat_step, NT)
                for t in range(NT):
                    dve.bn_aggr(m.moments[:, t, :], m.stats[:, t, :]).then_inc(stat_step, 1)
                dve.wait_ge(stat_step, 2 * NT)

        @block.scalar
        def _(act):
            if layer:
                normalise(None, act, m, step, root, True)
            for b in range(B):
                for h in range(CT):
                    act.wait_ge(turned, CT * b + h + 1)
                    if b >= 2:
                        act.wait_ge(y_made, TPB * (b - 1))
                    if layer:
                        ins = act.activation(m.xT[b % 2][:, h, :], m.bank[h], ACT.Silu,
                                             bias=m.mod1_shift[:, h, b:b + 1], scale=m.mod1_scale[:, h, b:b + 1])
                    else:
                        ins = act.activation(m.xT[b % 2][:, h, :], m.bank[h], ACT.Copy)
                    ins.then_inc(srcT_ready, 1)

        @block.tensor
        def _(pe):
            def turn(b):
                for h in range(CT):
                    if b:
                        pe.wait_ge(srcT_ready, CT * (b - 1) + h + 1)
                    for t in range(TPB):
                        if layer:
                            pe.wait_ge(src_ready, TPB * b + t + 1)
                        last = nc.tensor.transpose(m.bank[h][:, t * P:(t + 1) * P],
                                                   src[:, TPB * b + t, h * P:(h + 1) * P], m.ident[:, :])
                    last.then_inc(turned, 1)

            turn(0)
            for b in range(B):
                if b + 1 < B:
                    turn(b + 1)
                pe.wait_ge(srcT_ready, CT * (b + 1))
                for t in range(TPB):
                    n = TPB * b + t
                    if n >= 2:
                        pe.wait_ge(y_added, n - 1)
                    for k in range(CT):
                        last = nc.tensor.matmul(m.bank[2 + n % 2][:, 0:C], m.xT[b % 2][:, k, t * P:(t + 1) * P],
                                                w[:, k, :], start=(k == 0), stop=(k == CT - 1))
                    last.then_inc(y_made, 1)

        @block.sync
        def _(sp):
            if layer:
                for t in range(NT):
                    b, q = divmod(t, TPB)
                    sp.wait_ge(y_added, t + 1)
                    sp.dma_start(m.out[b, q * P:(q + 1) * P, :], m.y_out[t % 2][:, :])\
                        .then_inc(y_out_done[t % 2], 16)
                for done in y_out_done:
                    sp.wait_ge(done, 16 * NT // 2)


_INS = ["x", "cond_2048", "mask_BxS_ff1", "L0_cond_pos", "L0_cond_rms_w", "L0_cond_w_cond", "L0_cond_w_qkv", "L0_cond_w_out",
        "L1_cond_norm_w", "L1_cond_norm_b", "L1_cond_q_w", "L1_cond_q_b", "L1_cond_k_w", "L1_cond_k_b",
        "L1_cond_v_w", "L1_cond_v_b", "L1_cond_emb_w", "L1_cond_emb_b", "L1_cond_sb_norm_w",
        "L1_cond_sb_norm_b", "L1_cond_out_w", "L1_cond_out_b"]


def kernel(**inputs):
    import numpy as np
    import concourse.bacc as bacc
    from concourse.bass_utils import run_bass_kernel_spmd

    nc = bacc.Bacc("TRN2", target_bir_lowering=False, num_devices=1)
    arrays, args = {}, []
    for name in _INS:
        a = np.ascontiguousarray(inputs[name])
        arrays[f"in_{name}"] = a
        args.append(nc.dram_tensor(f"in_{name}", a.shape, mybir.dt.from_np(a.dtype), kind="ExternalInput").ap())
    args.append(nc.dram_tensor("y", (B, S, C), F32, kind="ExternalOutput").ap())
    build(nc, *args)
    r = run_bass_kernel_spmd(nc, [arrays], core_ids=[0])
    return r.results[0]["y"]
```

```python
from contextlib import ExitStack

import concourse.bass as bass
from concourse import mybir

F32 = mybir.dt.float32
F16 = mybir.dt.float16
ALU = mybir.AluOpType
ACT = mybir.ActivationFunctionType
AX = mybir.AxisListType

P = 128
B, S, C, H = 4, 512, 256, 16
DH = C // H
TPB = S // P
NT = B * TPB
CT = C // P
COND = 2 * C
KC = COND // P
G = 4
NG = H // G
W32 = 32
QT = TPB
KT = TPB
EXPS = KT * G
MAXES = G * QT
LEAD = 2

HIGH_LOW = [(0, 0), (0, 1), (1, 0), (1, 1)]
ROW_MASK = 4 * DH
ROW_SHIFT = 96
MASK_UNIT = 64.0
MASK_VALUE = 1e6

NORM_W, NORM_B, Q_B, K_B, SBN_W, SBN_B, EMB_B, MASK = 0, 2, 4, 6, 8, 10, 12, 16
VEC_ROWS = MASK + NT


class Buffers:
    pass


class RunAhead:
    pass


def build(nc, x, cond, mask, pos, rms_w, w_cond, w_qkv, w_out, norm_w, norm_b, q_w, q_b, k_w, k_b,
          v_w, v_b, emb_w, emb_b, sbn_w, sbn_b, out_w, out_b, out):
    m = Buffers()
    m.x, m.cond, m.mask, m.pos, m.out = x, cond, mask, pos, out
    m.rms_w, m.w_cond, m.w_qkv, m.w_out = rms_w, w_cond, w_qkv, w_out
    m.norm_w, m.norm_b, m.q_w, m.q_b, m.k_w, m.k_b, m.v_w, m.v_b = norm_w, norm_b, q_w, q_b, k_w, k_b, v_w, v_b
    m.emb_w, m.emb_b, m.sbn_w, m.sbn_b, m.out_w, m.out_b = emb_w, emb_b, sbn_w, sbn_b, out_w, out_b
    with ExitStack() as ctx:
        def sb(name, shape, dt=F32):
            return ctx.enter_context(nc.sbuf_tensor(name, shape, dt))

        m.bank = [ctx.enter_context(nc.psum_tensor(f"bank{i}", [P, 512], F32))[:, :] for i in range(8)]
        m.score_banks, m.max_banks, m.ACC, m.TURN = m.bank[0:2], m.bank[2:6], m.bank[6], m.bank[7]

        m.X = sb("X", [P, NT, C])
        m.V = sb("V", [P, NT, C])
        m.O = sb("O", [P, NT, C])
        m.XN = m.O
        m.xT = [sb(f"xT{i}", [P, CT, 512]) for i in range(2)]
        m.parts = [sb(f"parts{i}", [P, 2, 2 * CT, 512], F16) for i in range(2)]
        m.q_aug = [sb(f"q_aug{g}", [P, G, 512], F16) for g in range(NG)]
        m.k_aug = [sb(f"k_aug{g}", [P, G, 512], F16) for g in range(NG)]
        m.v_aug = [sb(f"v_aug{g}", [P, KT, G, W32]) for g in range(NG)]
        m.probs = [sb(f"probs{i}", [P, G, 512]) for i in range(KT)]
        m.oT = sb("oT", [P, 512])
        m.row_max = [sb(f"row_max{i}", [P, MAXES]) for i in range(2)]
        m.neg_max = [sb(f"neg_max{i}", [P, MAXES], F16) for i in range(2)]
        m.shift_rows = [sb(f"shift_rows{g}", [MAXES, P], F16) for g in range(NG)]
        m.inv_sum = sb("inv_sum", [P, QT, G, 1])

        m.wqkv = sb("wqkv", [P, CT, 3 * C])
        m.wo = sb("wo", [P, CT, C])
        m.wc = sb("wc", [P, KC, COND])
        m.wqkv1 = sb("wqkv1", [P, CT, 3 * C])
        m.wo1 = sb("wo1", [P, CT, C])
        m.vb_row = sb("vb_row", [P, C])
        m.ob_row = sb("ob_row", [P, C])
        m.ident = sb("ident", [P, P])
        m.ident16 = sb("ident16", [P, P], F16)
        m.vec_rows = sb("vec_rows", [VEC_ROWS, P])
        m.vec = sb("vec", [P, VEC_ROWS])
        m.rms_rows = sb("rms_rows", [CT, P])
        m.rms_vec = sb("rms_vec", [P, CT])
        m.cond_rows = sb("cond_rows", [B, COND])
        m.condT = sb("condT", [P, KC, B])
        m.ss_rows = sb("ss_rows", [B, COND])
        m.mod0_scale = sb("mod0_scale", [P, CT, B])
        m.mod0_shift = sb("mod0_shift", [P, CT, B])
        m.mod1 = sb("mod1", [P, KC, B])
        m.mod1_scale = sb("mod1_scale", [P, CT, B])
        m.mod1_shift = sb("mod1_shift", [P, CT, B])
        m.mask_row = sb("mask_row", [B, S])
        m.mask_hi = sb("mask_hi", [B, S], F16)
        m.mask_lo = sb("mask_lo", [B, S], F16)
        m.stats = sb("stats", [P, NT, 6])
        m.moments = sb("moments", [P, NT, 2])
        m.spread = sb("spread", [P, NT])
        m.rstd = sb("rstd", [P, NT])
        m.pos_rows = sb("pos_rows", [P, TPB, 2 * DH])
        m.sinT = sb("sinT", [P, S])
        m.cosT = sb("cosT", [P, S])
        m.rotate = sb("rotate", [P, P])
        m.plain, m.with_cos = ([m.probs[0][:, 2 * j + i, :] for i in range(2)] for j in range(2))
        m.roped = [m.probs[1][:, i, :] for i in range(2)]
        m.pos_wide = [m.probs[2][:, i, :] for i in range(2)]
        m.zeros = m.probs[3][:, 0:2, :].bitcast(F16).rearrange("p a (b n) -> p (a b) n", b=2)
        m.aug_fill = sb("aug_fill", [P, 2])
        m.v_tmp = [sb(f"v_tmp{i}", [P, C]) for i in range(2)]
        m.y_out = [sb(f"y_out{i}", [P, C]) for i in range(2)]

        m.qk_dram = nc.dram_tensor("qk_parts", [B, 2, 2, C, S], F16, kind="Internal").ap()
        m.mask_dram = nc.dram_tensor("mask_parts", [2, B, S], F16, kind="Internal").ap()

        for layer in range(2):
            with ExitStack() as shared:
                ahead = RunAhead()
                (ahead.row_scores_made, ahead.max_made, ahead.shift_made, ahead.shift_turned, ahead.shift_copied,
                 ahead.v_in) = sems(
                    shared, nc, f"ra{layer}", "row_scores_made", "max_made", "shift_made", "shift_turned",
                    "shift_copied", "v_in")
                ahead.operands_in = sems(shared, nc, f"ra{layer}", *[f"operands_in{g}" for g in range(NG)])
                ahead.shift_in = sems(shared, nc, f"ra{layer}", *[f"shift_in{g}" for g in range(NG)])
                project(nc, layer, m, ahead)
                attend(nc, layer, m, ahead)
            finish(nc, layer, m)


def sems(ctx, nc, tag, *names):
    return [ctx.enter_context(nc.semaphore(f"{tag}_{n}")) for n in names]


class Opening:
    pass


def opening(nc, m, own, step, root, xn_ready):
    (cond_in, wc_in, rms_ready, pos_in, wqkv_in, late_in, ident_made, fill_made, rotate_made, ones_made, q_scaled,
     zeros_made, aug_made, cond_turned, cond_ready, ss_made, ss_copied, ss_turned, mod_made, stat_step,
     pos_wide_made, pos_turned, pos_copied) = sems(
        own, nc, "op", "cond_in", "wc_in", "rms_ready", "pos_in", "wqkv_in", "late_in", "ident_made", "fill_made",
        "rotate_made", "ones_made", "q_scaled", "zeros_made", "aug_made", "cond_turned", "cond_ready", "ss_made",
        "ss_copied", "ss_turned", "mod_made", "stat_step", "pos_wide_made", "pos_turned", "pos_copied")
    x_in = sems(own, nc, "op", *[f"x_in{b}" for b in range(B)])
    POS_BANKS, SS_TURNED, SS, COND = (4, 5), 3, 6, 7
    rows = [(NORM_W, m.norm_w), (NORM_B, m.norm_b), (Q_B, m.q_b), (K_B, m.k_b),
            (SBN_W, m.sbn_w), (SBN_B, m.sbn_b), (EMB_B, m.emb_b)]
    o = Opening()
    o.mod_made, o.rotate_made, o.q_scaled, o.pos_copied, o.aug_made = (
        mod_made, rotate_made, q_scaled, pos_copied, aug_made)

    def sync(sp):
        def load_x(b):
            sp.dma_start(m.X[:, b * TPB:(b + 1) * TPB, :], m.x[b].rearrange("(t p) c -> p t c", p=P))\
                .then_inc(x_in[b], 16)

        sp.dma_start(m.cond_rows[:, :], m.cond).then_inc(cond_in, 16)
        sp.dma_start(m.rms_rows[:, :], m.rms_w.rearrange("(a p) -> a p", p=P)).then_inc(cond_in, 16)
        load_x(0)
        sp.dma_start(m.pos_rows[:, :, :], m.pos.rearrange("(t p) o d -> p t (o d)", p=P)).then_inc(pos_in, 16)
        for b in range(1, B):
            load_x(b)
        for at, v in rows:
            n = v.shape[0] // P
            sp.dma_start(m.vec_rows[at:at + n, :], v.rearrange("(a p) -> a p", p=P)).then_inc(late_in, 16)
        sp.dma_start(m.vec_rows[MASK:MASK + NT, :], m.mask.rearrange("b (t p) -> (b t) p", p=P))\
            .then_inc(late_in, 16)
        sp.dma_start(m.mask_row[:, :], m.mask).then_inc(late_in, 16)
        sp.wait_ge(ss_made, 1)
        sp.dma_start(m.wc[:, :, :], m.emb_w.rearrange("(k p) n -> p k n", p=P)).then_inc(late_in, 16)

    def sync_end(sp):
        sp.wait_ge(late_in, 16 * (len(rows) + 3 + 7))

    def scalar(act):
        act.dma_start(m.wc[:, :, :], m.w_cond.rearrange("(k p) n -> p k n", p=P)).then_inc(wc_in, 16)
        act.dma_start(m.wqkv[:, :, :], m.w_qkv.rearrange("(k p) n -> p k n", p=P)).then_inc(wqkv_in, 16)
        for i, w in enumerate((m.q_w, m.k_w, m.v_w)):
            act.dma_start(m.wqkv1[:, :, i * C:(i + 1) * C], w.rearrange("(k p) n -> p k n", p=P))\
                .then_inc(late_in, 16)
        for to, w in ((m.wo, m.w_out), (m.wo1, m.out_w)):
            act.dma_start(to[:, :, :], w.rearrange("(k p) n -> p k n", p=P)).then_inc(late_in, 16)
        for to, v in ((m.vb_row, m.v_b), (m.ob_row, m.out_b)):
            act.dma_start(to[:, :], v.partition_broadcast(P)).then_inc(late_in, 16)
        normalise(None, act, m, step, root, False, 0, 0, TPB)
        normalise(None, act, m, step, root, False, 1, TPB, NT)

    def gpsimd(pool):
        pool.memset(m.ident[:, :], 0.0).then_inc(ident_made, 1)
        pool.memset(m.ident16[:, :], 0.0).then_inc(ident_made, 1)
        pool.memset(m.rotate[:, :], 0.0).then_inc(rotate_made, 1)
        pool.memset(m.aug_fill[:, :], 0.0).then_inc(fill_made, 1)
        for n, t in enumerate((m.ident, m.ident16)):
            pool.wait_ge(ident_made, 2 + n)
            pool.affine_select(out=t[:, :], in_=t[:, :], compare_op=ALU.not_equal, fill=1.0, base=0,
                               pattern=[[-1, P]], channel_multiplier=1).then_inc(ident_made, 1)
        for n, (col, row, value) in enumerate([(0, ROW_MASK, MASK_UNIT), (0, ROW_MASK + 1, MASK_UNIT),
                                               (1, ROW_SHIFT, 1.0)]):
            pool.wait_ge(fill_made, 1 + n)
            at = m.aug_fill[:, col:col + 1]
            pool.affine_select(out=at, in_=at, compare_op=ALU.not_equal, fill=value, base=-row,
                               pattern=[[0, 1]], channel_multiplier=1).then_inc(fill_made, 1)
        pool.wait_ge(rotate_made, 1)
        halves = m.rotate[:, :].rearrange("p (h two d) -> p h two d", two=2, d=DH // 2)
        for half, (base, value) in enumerate([(-DH // 2, -1.0), (0, 1.0)]):
            pool.affine_select(out=halves[:, :, half, :], in_=halves[:, :, half, :], compare_op=ALU.not_equal,
                               fill=value, base=base, pattern=[[-DH, P // DH], [-1, DH // 2]],
                               channel_multiplier=1).then_inc(rotate_made, 1)
        pool.wait_ge(wqkv_in, 16)
        pool.tensor_scalar(m.wqkv[:, :, 0:C], m.wqkv[:, :, 0:C], float(DH) ** -0.5, None, ALU.mult)\
            .then_inc(q_scaled, 1)
        for g in range(NG):
            pool.memset(m.v_aug[g][:, :, :, DH:W32], 0.0).then_inc(ones_made, 1)
        pool.wait_ge(ones_made, NG)
        for g in range(NG):
            pool.memset(m.v_aug[g][:, :, :, DH:DH + 1], 1.0).then_inc(ones_made, 1)
        pool.wait_ge(ones_made, 2 * NG)
        pool.wait_ge(q_scaled, 1)

    def tensor(pe):
        pe.wait_ge(ident_made, 4)
        pe.wait_ge(cond_in, 32)
        nc.tensor.transpose(m.bank[COND][:, KC * B:KC * B + CT], m.rms_rows[:, :], m.ident[0:CT, 0:CT])
        for k in range(KC):
            last = nc.tensor.transpose(m.bank[COND][:, k * B:(k + 1) * B], m.cond_rows[:, k * P:(k + 1) * P],
                                       m.ident[0:B, 0:B])
        last.then_inc(cond_turned, 1)
        pe.wait_ge(cond_ready, 1)
        pe.wait_ge(wc_in, 16)
        for k in range(KC):
            last = nc.tensor.matmul(m.bank[SS][0:B, :], m.condT[:, k, :], m.wc[:, k, :],
                                    start=(k == 0), stop=(k == KC - 1))
        last.then_inc(ss_made, 1)

    def tensor_ss(pe):
        pe.wait_ge(ss_copied, 1)
        for k in range(KC):
            last = nc.tensor.transpose(m.bank[SS_TURNED][:, k * B:(k + 1) * B], m.ss_rows[:, k * P:(k + 1) * P],
                                       m.ident[0:B, 0:B])
        last.then_inc(ss_turned, 1)

    def tensor_pos(pe):
        pe.wait_ge(pos_wide_made, 2)
        for i in range(2):
            for t in range(TPB):
                last = nc.tensor.transpose(m.bank[POS_BANKS[i]][:, t * P:(t + 1) * P],
                                           m.pos_wide[i][:, t * P:(t + 1) * P], m.ident[:, :])
        last.then_inc(pos_turned, 1)

    def stats(dve, b):
        dve.wait_ge(x_in[b], 16)
        for t in range(TPB * b, TPB * (b + 1)):
            dve.bn_stats(m.stats[:, t, :], m.X[:, t, :]).then_inc(stat_step, 1)

    def vector(dve):
        dve.memset(m.zeros, 0.0).then_inc(zeros_made, 1)
        dve.wait_ge(cond_turned, 1)
        dve.tensor_copy(m.condT[:, :, :], m.bank[COND][:, 0:KC * B].rearrange("p (k b) -> p k b", b=B))\
            .then_inc(cond_ready, 1)
        dve.tensor_copy(m.rms_vec[:, :], m.bank[COND][:, KC * B:KC * B + CT]).then_inc(rms_ready, 1)
        stats(dve, 0)
        dve.wait_ge(stat_step, TPB)
        for t in range(TPB):
            dve.bn_aggr(m.moments[:, t, :], m.stats[:, t, :]).then_inc(stat_step, 1)
        dve.wait_ge(stat_step, 2 * TPB)
        dve.wait_ge(pos_in, 16)
        both = m.pos_rows[:, :, :].rearrange("p t (d two) -> p t two d", two=2)
        for i in range(2):
            dve.tensor_copy(m.pos_wide[i].rearrange("p (t h d) -> p t h d", t=TPB, d=DH),
                            both[:, :, i:i + 1, :].broadcast_to([P, TPB, P // DH, DH])).then_inc(pos_wide_made, 1)
        normalise(dve, None, m, step, root, False, 0, 0, TPB)
        for t in range(TPB):
            normal_tile(dve, m, m.X, t, False).then_inc(xn_ready, 1)
        dve.wait_ge(ss_made, 1)
        dve.tensor_copy(m.ss_rows[:, :], m.bank[SS][0:B, :]).then_inc(ss_copied, 1)
        dve.wait_ge(ss_turned, 1)
        dve.wait_ge(rms_ready, 1)
        ss = m.bank[SS_TURNED][:, 0:KC * B].rearrange("p (k b) -> p k b", b=B)
        for h in range(CT):
            dve.tensor_scalar(m.mod0_scale[:, h, :], ss[:, h, :], 1.0, m.rms_vec[:, h:h + 1],
                              ALU.add, ALU.mult).then_inc(mod_made, 1)
        dve.tensor_copy(m.mod0_shift[:, :, :], ss[:, CT:2 * CT, :]).then_inc(mod_made, 1)
        dve.wait_ge(pos_turned, 1)
        for to, bank in ((m.sinT, POS_BANKS[0]), (m.cosT, POS_BANKS[1])):
            dve.tensor_copy(to[:, :], m.bank[bank]).then_inc(pos_copied, 1)
        dve.wait_ge(pos_copied, 2)
        for b in range(1, B):
            stats(dve, b)
        done = 2 * TPB
        dve.wait_ge(stat_step, done + NT - TPB)
        for t in range(TPB, NT):
            dve.bn_aggr(m.moments[:, t, :], m.stats[:, t, :]).then_inc(stat_step, 1)
        dve.wait_ge(stat_step, 2 * NT)
        normalise(dve, None, m, step, root, False, 1, TPB, NT)
        for t in range(TPB, NT):
            normal_tile(dve, m, m.X, t, False).then_inc(xn_ready, 1)

    def fill(dve, g):
        if g == 0:
            dve.wait_ge(zeros_made, 1)
            dve.wait_ge(fill_made, 4)
        for i, aug in enumerate((m.q_aug, m.k_aug)):
            dve.tensor_scalar(aug[g][:, :, :], m.zeros, m.aug_fill[:, i:i + 1], None, ALU.add).then_inc(aug_made, 1)

    o.sync, o.sync_end, o.scalar, o.gpsimd, o.tensor, o.tensor_ss, o.tensor_pos, o.vector, o.fill = (
        sync, sync_end, scalar, gpsimd, tensor, tensor_ss, tensor_pos, vector, fill)
    return o


def normalise(dve, act, m, step, root, centred, chain=0, t0=0, t1=NT):
    spread, rstd, mean, var = m.spread[:, t0:t1], m.rstd[:, t0:t1], m.moments[:, t0:t1, 0], m.moments[:, t0:t1, 1]
    steps = 2 if centred else 3
    at = steps * chain
    if dve is not None:
        if centred:
            dve.tensor_scalar(spread, var, 1e-5, None, ALU.add).then_inc(step, 1)
        else:
            dve.tensor_tensor(rstd, mean, mean, ALU.mult).then_inc(step, 1)
            dve.wait_ge(step, at + 1)
            dve.scalar_tensor_tensor(spread, var, 1e-6, rstd, ALU.add, ALU.add).then_inc(step, 1)
        dve.wait_ge(root, chain + 1)
        dve.reciprocal(rstd, spread).then_inc(step, 1)
        dve.wait_ge(step, at + steps)
    if act is not None:
        act.wait_ge(step, at + steps - 1)
        act.activation(spread, spread, ACT.Sqrt).then_inc(root, 1)


def normal_tile(dve, m, src, t, centred):
    if centred:
        return dve.tensor_scalar(m.XN[:, t, :], src[:, t, :], m.moments[:, t, 0:1], m.rstd[:, t:t + 1],
                                 ALU.subtract, ALU.mult)
    return dve.tensor_scalar(m.XN[:, t, :], src[:, t, :], m.rstd[:, t:t + 1], None, ALU.mult)


def load_operands(sp, m, layer, b, g, done):
    for r, (qp, kp) in enumerate(HIGH_LOW):
        for aug, side, part in ((m.q_aug, 0, qp), (m.k_aug, 1, kp)):
            sp.dma_start(aug[g][r * DH:(r + 1) * DH, :, :],
                         m.qk_dram[b, side, part, g * G * DH:(g + 1) * G * DH, :]
                         .rearrange("(h d) t -> d h t", d=DH)).then_inc(done, 16)
    if layer:
        for part in range(2):
            row = ROW_MASK + part
            sp.dma_start(m.k_aug[g][row:row + 1, :, :],
                         m.mask_dram[part, bass.ds(b, 1), :].unsqueeze(1).broadcast_to([1, G, S])).then_inc(done, 16)


def loads_of(layer):
    return 2 * len(HIGH_LOW) + 2 * layer


def group_values(pool, m, b, g):
    return pool.tensor_copy(m.v_aug[g][:, :, :, 0:DH],
                            m.V[:, bass.ds(b * TPB, TPB), g * G * DH:(g + 1) * G * DH]
                            .rearrange("p t (h d) -> p t h d", d=DH))


def row_score_tile(nc, m, g, j, bank):
    h, q = divmod(j, QT)
    return nc.tensor.matmul(bank, m.q_aug[g][0:ROW_SHIFT, h, q * P:(q + 1) * P],
                            m.k_aug[g][0:ROW_SHIFT, h, :], start=True, stop=True)


def project(nc, layer, m, ahead):
    w = m.wqkv1 if layer else m.wqkv
    with ExitStack() as own:
        (step, root, xn_ready, x_turned, xT_ready, qk_made, plain_ready, rotated, sin_done, cos_done, rope_done,
         high_made, low_made, v_made, v_read, v_ready) = sems(
            own, nc, f"pr{layer}", "step", "root", "xn_ready", "x_turned", "xT_ready", "qk_made", "plain_ready",
            "rotated", "sin_done", "cos_done", "rope_done", "high_made", "low_made", "v_made", "v_read",
            "v_ready")
        parts_out = sems(own, nc, f"pr{layer}", *[f"parts_out{i}" for i in range(4 * CT)])
        start = None if layer else opening(nc, m, own, step, root, xn_ready)
        NQ = 2 * CT
        PRODUCTS = NQ + TPB
        TURN_BANKS, QK_BANKS, V_BANKS, ROT_BANKS = (0, 1), (2, 3), (4, 5), (6, 7)
        FIRST_ROWS = B - LEAD
        ROWS = MAXES // PRODUCTS
        SHIFT_AT = 1
        turn16 = m.bank[TURN_BANKS[0]].bitcast(F16)

        def rows_with(b, i):
            if b < FIRST_ROWS:
                return range(0)
            n = ROWS * (PRODUCTS * (b - FIRST_ROWS) + i)
            return range(n, n + ROWS)

        def part(n, hl):
            return m.parts[n // NQ % 2][:, hl, n % NQ, :]

        def bias(n):
            at = (Q_B if n % NQ < CT else K_B) + n % CT
            return m.vec[:, at:at + 1]

        def parts_free(engine, n):
            if n >= 2 * NQ:
                engine.wait_ge(parts_out[n % (2 * NQ)], 16 * (n // (2 * NQ)))

        block = own.enter_context(nc.Block())

        @block.vector
        def _(dve):
            if layer:
                normalise(dve, None, m, step, root, True)
                for t in range(NT):
                    normal_tile(dve, m, m.X, t, True).then_inc(xn_ready, 1)
            else:
                start.vector(dve)

            def rope(n):
                f = m.roped[n % 2][:, :]
                dve.wait_ge(rotated, n + 1)
                if n >= 2:
                    dve.wait_ge(high_made, n - 1)
                    dve.wait_ge(low_made, n - 1)
                dve.tensor_tensor(f, m.bank[ROT_BANKS[n % 2]], m.sinT[:, :], ALU.mult).then_inc(sin_done, 1)
                dve.wait_ge(sin_done, n + 1)
                dve.wait_ge(cos_done, n + 1)
                dve.tensor_tensor(f, f, m.with_cos[n % 2][:, :], ALU.add).then_inc(rope_done, 1)

            def low(n):
                dve.wait_ge(high_made, n + 1)
                parts_free(dve, n)
                if layer:
                    ins = dve.scalar_tensor_tensor(part(n, 1), m.bank[QK_BANKS[n % 2]], bias(n), part(n, 0),
                                                   ALU.add, ALU.subtract)
                else:
                    ins = dve.tensor_tensor(part(n, 1), m.roped[n % 2][:, :], part(n, 0), ALU.subtract)
                ins.then_inc(low_made, 1)

            def v_bias(n):
                dve.wait_ge(v_made, n + 1)
                if n >= 2:
                    dve.wait_ge(v_ready, n - 1)
                dve.tensor_tensor(m.v_tmp[n % 2][:, :], m.bank[V_BANKS[n % 2]][:, 0:C], m.vb_row[:, :],
                                  ALU.add).then_inc(v_read, 1)

            def maxima(b, i):
                for n in rows_with(b, i):
                    g, j = divmod(n, MAXES)
                    dve.wait_ge(ahead.row_scores_made, n + 1)
                    dve.tensor_reduce(m.row_max[g][:, j:j + 1], m.bank[TURN_BANKS[n % 2]], AX.X, ALU.max)\
                       .then_inc(ahead.max_made, 1)
                    if j == MAXES - 1:
                        dve.wait_ge(ahead.max_made, n + 1)
                        dve.tensor_scalar(m.neg_max[g][:, :], m.row_max[g][:, :], -1.0, None, ALU.mult)\
                           .then_inc(ahead.shift_made, 1)

            for b in range(B):
                for i in range(NQ):
                    n = NQ * b + i
                    if layer:
                        low(n)
                        maxima(b, i)
                    else:
                        if i == NQ - 1:
                            maxima(b, i)
                        if i:
                            rope(n - 1)
                        if i > 1:
                            low(n - 2)
                        if i < NQ - 1:
                            maxima(b, i)
                if not layer:
                    rope(NQ * b + NQ - 1)
                    low(NQ * b + NQ - 2)
                for t in range(TPB):
                    if layer:
                        v_bias(TPB * b + t)
                    maxima(b, NQ + t)
                    if not layer and t == 1:
                        low(NQ * b + NQ - 1)
                    if not layer and b == 0:
                        start.fill(dve, t)
            dve.wait_ge(ahead.shift_made, LEAD)

        @block.scalar
        def _(act):
            if layer:
                normalise(None, act, m, step, root, True)
            else:
                start.scalar(act)
                act.wait_ge(start.mod_made, CT + 1)

            def turn(b):
                for h in range(CT):
                    act.wait_ge(x_turned, CT * b + h + 1)
                    if b >= 2:
                        act.wait_ge(v_made, TPB * (b - 1))
                    if layer:
                        scale, shift = m.vec[:, NORM_W + h:NORM_W + h + 1], m.vec[:, NORM_B + h:NORM_B + h + 1]
                    else:
                        scale, shift = m.mod0_scale[:, h, b:b + 1], m.mod0_shift[:, h, b:b + 1]
                    act.activation(m.xT[b % 2][:, h, :], m.bank[h], ACT.Identity, bias=shift, scale=scale)\
                        .then_inc(xT_ready, 1)

            def plain(n):
                act.wait_ge(qk_made, n + 1)
                if n >= 2:
                    act.wait_ge(rotated, n - 1)
                    act.wait_ge(cos_done, n - 1)
                act.activation(m.plain[n % 2][:, :], m.bank[QK_BANKS[n % 2]], ACT.Copy).then_inc(plain_ready, 1)

            def high(n):
                parts_free(act, n)
                if layer:
                    act.wait_ge(qk_made, n + 1)
                    ins = act.activation(part(n, 0), m.bank[QK_BANKS[n % 2]], ACT.Identity, bias=bias(n))
                else:
                    act.wait_ge(rope_done, n + 1)
                    ins = act.activation(part(n, 0), m.roped[n % 2][:, :], ACT.Copy)
                ins.then_inc(high_made, 1)

            turn(0)
            for b in range(B):
                for i in range(NQ):
                    n = NQ * b + i
                    if layer:
                        high(n)
                    else:
                        plain(n)
                        if i:
                            high(n - 1)
                    if b == B - 1 and i == SHIFT_AT:
                        act.wait_ge(ahead.shift_turned, 1)
                        act.activation(m.shift_rows[0][:, :], turn16[0:MAXES, 0:P], ACT.Copy)\
                            .then_inc(ahead.shift_copied, 1)
                if b + 1 < B:
                    turn(b + 1)
                if not layer:
                    for t in range(TPB * b, TPB * (b + 1)):
                        act.wait_ge(v_made, t + 1)
                        act.activation(m.V[:, t, :], m.bank[V_BANKS[t % 2]][:, 0:C], ACT.Copy).then_inc(v_read, 1)
                        if t % TPB == 1:
                            high(NQ * b + NQ - 1)

        @block.gpsimd
        def _(pool):
            if not layer:
                start.gpsimd(pool)
                pool.wait_ge(start.pos_copied, 2)
            if layer:
                for n in range(NT):
                    pool.wait_ge(v_read, n + 1)
                    pool.tensor_scalar(m.V[:, n, :], m.v_tmp[n % 2][:, :], m.vec[:, MASK + n:MASK + n + 1], None,
                                       ALU.mult).then_inc(v_ready, 1)
                    if TPB <= n < TPB + NG:
                        pool.wait_ge(v_ready, TPB)
                        group_values(pool, m, 0, n - TPB).then_inc(ahead.v_in, 1)
            else:
                for n in range(NQ * B):
                    pool.wait_ge(plain_ready, n + 1)
                    if n >= 2:
                        pool.wait_ge(rope_done, n - 1)
                    pool.tensor_tensor(m.with_cos[n % 2][:, :], m.plain[n % 2][:, :], m.cosT[:, :], ALU.mult)\
                        .then_inc(cos_done, 1)
                    if NQ < n <= NQ + NG:
                        pool.wait_ge(v_read, TPB)
                        group_values(pool, m, 0, n - NQ - 1).then_inc(ahead.v_in, 1)
            pool.wait_ge(ahead.v_in, NG)

        @block.tensor
        def _(pe):
            def turn(b):
                for h in range(CT):
                    if b:
                        pe.wait_ge(xT_ready, CT * (b - 1) + h + 1)
                    if b > FIRST_ROWS:
                        pe.wait_ge(ahead.max_made, rows_with(b - 1, NQ).start - 1 + h)
                    for t in range(TPB):
                        pe.wait_ge(xn_ready, TPB * b + t + 1)
                        last = nc.tensor.transpose(m.bank[h][:, t * P:(t + 1) * P],
                                                   m.XN[:, TPB * b + t, h * P:(h + 1) * P], m.ident[:, :])
                    last.then_inc(x_turned, 1)

            def queries_keys(n):
                if n >= 2:
                    pe.wait_ge(low_made if layer else plain_ready, n - 1)
                i = n % NQ
                for k in range(CT):
                    last = nc.tensor.matmul(m.bank[QK_BANKS[n % 2]], w[:, k, i * P:(i + 1) * P],
                                            m.xT[n // NQ % 2][:, k, :], start=(k == 0), stop=(k == CT - 1))
                last.then_inc(qk_made, 1)

            def rotate(n):
                pe.wait_ge(plain_ready, n + 1)
                if n >= 2:
                    pe.wait_ge(sin_done, n - 1)
                nc.tensor.matmul(m.bank[ROT_BANKS[n % 2]], m.rotate[:, :], m.plain[n % 2][:, :],
                                 start=True, stop=True).then_inc(rotated, 1)

            def row_scores(b, i):
                for n in rows_with(b, i):
                    g, j = divmod(n, MAXES)
                    if j == 0:
                        pe.wait_ge(ahead.operands_in[g], 16 * loads_of(layer))
                    if i >= NQ and b + 1 < B:
                        pe.wait_ge(xT_ready, CT * (b + 2))
                    if n >= 2:
                        pe.wait_ge(ahead.max_made, n - 1)
                    if b == B - 1 and i == SHIFT_AT + 1:
                        pe.wait_ge(ahead.shift_copied, 1)
                    row_score_tile(nc, m, g, j, m.bank[TURN_BANKS[n % 2]]).then_inc(ahead.row_scores_made, 1)

            if layer:
                turn(0)
            else:
                start.tensor(pe)
                turn(0)
                start.tensor_ss(pe)
                start.tensor_pos(pe)
                pe.wait_ge(start.q_scaled, 1)
                pe.wait_ge(start.rotate_made, 3)
            for b in range(B):
                pe.wait_ge(xT_ready, CT * (b + 1))
                for i in range(NQ):
                    queries_keys(NQ * b + i)
                    if i and not layer:
                        rotate(NQ * b + i - 1)
                    row_scores(b, i)
                    if b == B - 1 and i == SHIFT_AT:
                        pe.wait_ge(ahead.shift_made, 1)
                        pe.wait_ge(ahead.max_made, rows_with(b, i).stop - 1)
                        nc.tensor.transpose(turn16[0:MAXES, 0:P], m.neg_max[0][:, :], m.ident16[:, :])\
                            .then_inc(ahead.shift_turned, 1)
                if b + 1 < B:
                    turn(b + 1)
                if not layer:
                    rotate(NQ * b + NQ - 1)
                for t in range(TPB):
                    n = TPB * b + t
                    if n >= 2:
                        pe.wait_ge(v_read, n - 1)
                    elif not layer:
                        pe.wait_ge(start.pos_copied, 2)
                    for k in range(CT):
                        last = nc.tensor.matmul(m.bank[V_BANKS[n % 2]][:, 0:C], m.xT[b % 2][:, k, t * P:(t + 1) * P],
                                                w[:, k, 2 * C:3 * C], start=(k == 0), stop=(k == CT - 1))
                    last.then_inc(v_made, 1)
                    row_scores(b, NQ + t)

        @block.sync
        def _(sp):
            if not layer:
                start.sync(sp)
            for n in range(NQ * B):
                b, i = divmod(n, NQ)
                sp.wait_ge(low_made, n + 1)
                sp.dma_start(m.qk_dram[b, i // CT, :, (i % CT) * P:(i % CT + 1) * P, :]
                             .rearrange("l p t -> p l t"), m.parts[b % 2][:, :, i, :])\
                    .then_inc(parts_out[n % (2 * NQ)], 16)
                if b == 1:
                    if i == 0:
                        for out in parts_out[0:NQ]:
                            sp.wait_ge(out, 16)
                        if not layer:
                            sp.wait_ge(start.aug_made, 2 * NG)
                    load_operands(sp, m, layer, 0, i, ahead.operands_in[i])
            sp.wait_ge(ahead.shift_copied, 1)
            sp.dma_start(m.q_aug[0][ROW_SHIFT:ROW_SHIFT + 1, :, :], m.shift_rows[0][:, :])\
                .then_inc(ahead.shift_in[0], 16)
            sp.wait_ge(ahead.shift_in[0], 16)
            for loaded in ahead.operands_in:
                sp.wait_ge(loaded, 16 * loads_of(layer))
            for out in parts_out:
                sp.wait_ge(out, 16 * B // 2)
            if not layer:
                start.sync_end(sp)


def attend(nc, layer, m, ahead):
    LOADS = loads_of(layer)
    with ExitStack() as own:
        (scores_made, exp_made, probs_used, acc_copied, o_turned, o_written, inv_made, stat_made) = sems(
            own, nc, f"at{layer}", "scores_made", "exp_made", "probs_used", "acc_copied", "o_turned",
            "o_written", "inv_made", "stat_made")
        block = own.enter_context(nc.Block())
        turn16 = m.TURN.bitcast(F16)

        def after(b, g, groups):
            return b + (g + groups) // NG, (g + groups) % NG

        def batches(engine, body):
            with engine.Fori(0, B - 1) as b:
                body(b, False)
            body(B - 1, True)

        @block.sync
        def _(sp):
            def shift(b, g):
                sp.wait_ge(ahead.shift_copied, b * NG + g + 1)
                sp.dma_start(m.q_aug[g][ROW_SHIFT:ROW_SHIFT + 1, :, :], m.shift_rows[g][:, :])\
                    .then_inc(ahead.shift_in[g], 16)

            def body(b, last):
                for g in range(NG):
                    s = b * NG + g
                    if not (last and g == NG - 1):
                        shift(*after(b, g, 1))
                    if not last:
                        sp.wait_ge(scores_made, EXPS * (s + 1))
                        load_operands(sp, m, layer, b + 1, g, ahead.operands_in[g])

            batches(sp, body)

        @block.gpsimd
        def _(pool):
            def body(b, last):
                if last:
                    return
                for g in range(NG):
                    s = b * NG + g
                    pool.wait_ge(probs_used, KT + KT * (s + 1))
                    group_values(pool, m, b + 1, g).then_inc(ahead.v_in, 1)

            batches(pool, body)

        @block.tensor
        def _(pe):
            def row_scores(b, g, j):
                if j == 0:
                    pe.wait_ge(ahead.operands_in[g], 16 * LOADS * (b + 1))
                pe.wait_ge(ahead.max_made, MAXES * (b * NG + g) + j - 3)
                row_score_tile(nc, m, g, j, m.max_banks[j % 4]).then_inc(ahead.row_scores_made, 1)

            def turn_shift(s, g, turned):
                pe.wait_ge(ahead.shift_made, s + 1)
                pe.wait_ge(o_written, 1 + turned)
                nc.tensor.transpose(turn16[0:MAXES, 0:P], m.neg_max[g % 2][:, :], m.ident16[:, :])\
                    .then_inc(ahead.shift_turned, 1)

            def scores(b, g, k, h):
                if k == 0 and h == 0:
                    pe.wait_ge(ahead.shift_in[g], 16 * (b + 1))
                pe.wait_ge(exp_made, EXPS * (b * NG + g) + G * k + h + 1)
                nc.tensor.matmul(m.score_banks[h % 2], m.k_aug[g][0:ROW_SHIFT + 1, h, k * P:(k + 1) * P],
                                 m.q_aug[g][0:ROW_SHIFT + 1, h, :], start=True, stop=True)\
                    .then_inc(scores_made, 1)

            def values(s, g, k, half):
                if k == 0 and half == 0:
                    pe.wait_ge(ahead.v_in, s + 1)
                    pe.wait_ge(acc_copied, 1 + s)
                pe.wait_ge(exp_made, 2 + EXPS * s + G * (k + 1))
                at = slice(half * S // 2, (half + 1) * S // 2)
                for h in range(G):
                    last = nc.tensor.matmul(m.ACC[W32 * h:W32 * (h + 1), at], m.v_aug[g][:, k, h, :],
                                            m.probs[k][:, h, at], start=(k == 0 and half == 0), stop=(k == KT - 1),
                                            tile_position=(0, W32 * h), skip_group_check=True)
                if half == 1:
                    last.then_inc(probs_used, 1)

            def turn_output(s, shifts):
                pe.wait_ge(acc_copied, 1 + s + 1)
                pe.wait_ge(ahead.shift_copied, shifts)
                pe.wait_ge(o_written, 1 + s)
                for q in range(QT):
                    last = nc.tensor.transpose(m.TURN[:, q * P:(q + 1) * P], m.oT[:, q * P:(q + 1) * P],
                                               m.ident[:, :])
                last.then_inc(o_turned, 1)

            def body(b, last):
                for g in range(NG):
                    s = b * NG + g
                    more = not (last and g >= NG - LEAD)
                    final = last and g == NG - 1
                    for k in range(KT):
                        for h in range(G):
                            scores(b, g, k, h)
                            if more:
                                row_scores(*after(b, g, LEAD), G * k + h)
                            if h % 2 and k > 0:
                                values(s, g, k - 1, h // 2)
                            if h % 2 and k == 0 and g > 0:
                                values(s - 1, g - 1, KT - 1, h // 2)
                        if k == 1 and not final:
                            turn_shift(s + 1, (g + 1) % NG, s if g == 0 else s - 1)
                        if k == 2 and g > 0:
                            turn_output(s - 1, s + 2 - (1 if final else 0))
                for half in range(2):
                    values(b * NG + NG - 1, NG - 1, KT - 1, half)
                turn_output(b * NG + NG - 1, b * NG + NG + (0 if last else 1))

            batches(pe, body)

        @block.scalar
        def _(act):
            act.sem_inc(exp_made, 2)
            act.sem_inc(probs_used, KT)
            act.sem_inc(acc_copied, 1)
            act.sem_inc(o_turned, 1)
            act.sem_inc(o_written, 1)
            def copy_shift(b, g):
                act.wait_ge(ahead.shift_turned, b * NG + g + 1)
                act.activation(m.shift_rows[g][:, :], turn16[0:MAXES, 0:P], ACT.Copy).then_inc(ahead.shift_copied, 1)

            def copy_output(s):
                act.wait_ge(probs_used, KT + KT * (s + 1))
                act.wait_ge(o_turned, 1 + s)
                act.activation(m.oT[:, :], m.ACC, ACT.Copy).then_inc(acc_copied, 1)

            def body(b, last):
                for g in range(NG):
                    s = b * NG + g
                    for k in range(KT):
                        for h in range(G):
                            act.wait_ge(scores_made, EXPS * s + G * k + h + 1)
                            if h == 0:
                                act.wait_ge(probs_used, KT * s + k + 1)
                            act.activation(m.probs[k][:, h, :], m.score_banks[h % 2], ACT.Exp)\
                                .then_inc(exp_made, 1)
                        if k == 0 and g > 0:
                            copy_output(s - 1)
                        if k == 1 and not (last and g == NG - 1):
                            copy_shift(*after(b, g, 1))
                copy_output(b * NG + NG - 1)

            batches(act, body)

        @block.vector
        def _(dve):
            def maximum(s, g, j):
                dve.wait_ge(ahead.row_scores_made, MAXES * s + j + 1)
                if j == 0:
                    dve.wait_ge(ahead.shift_made, s - 1)
                dve.tensor_reduce(m.row_max[g % 2][:, j:j + 1], m.max_banks[j % 4], AX.X, ALU.max)\
                    .then_inc(ahead.max_made, 1)

            def negate(s, g):
                dve.wait_ge(ahead.max_made, MAXES * (s + 1))
                dve.wait_ge(ahead.shift_turned, s - 1)
                dve.tensor_scalar(m.neg_max[g % 2][:, :], m.row_max[g % 2][:, :], -1.0, None, ALU.mult)\
                    .then_inc(ahead.shift_made, 1)

            def write_output(b, g):
                s = b * NG + g
                turned = m.TURN.rearrange("p (q h w) -> p q h w", q=QT, h=G)
                dve.wait_ge(o_turned, 1 + s + 1)
                dve.wait_ge(o_written, 1 + s)
                dve.reciprocal(m.inv_sum[:, :, :, :], turned[:, :, :, DH:DH + 1]).then_inc(inv_made, 1)
                dve.wait_ge(inv_made, s + 1)
                dve.tensor_tensor(m.O[:, bass.ds(b * TPB, TPB), g * G * DH:(g + 1) * G * DH]
                                  .rearrange("p t (h d) -> p t h d", d=DH),
                                  turned[:, :, :, 0:DH], m.inv_sum[:, :, :, :].broadcast_to([P, QT, G, DH]),
                                  ALU.mult).then_inc(o_written, 1)

            def body(b, last):
                for g in range(NG):
                    s = b * NG + g
                    more = not (last and g >= NG - LEAD)
                    for j in range(MAXES):
                        if more:
                            maximum(s + LEAD, (g + LEAD) % NG, j)
                        if j == 3 * QT + 1 and g > 0:
                            write_output(b, g - 1)
                    if more:
                        negate(s + LEAD, (g + LEAD) % NG)
                write_output(b, NG - 1)
                if layer:
                    dve.wait_ge(o_written, 1 + b * NG + NG)
                    for t in range(TPB):
                        dve.bn_stats(m.stats[:, bass.ds(b * TPB + t, 1), :].rearrange("p one s -> p (one s)"),
                                     m.O[:, bass.ds(b * TPB + t, 1), :].rearrange("p one c -> p (one c)"))\
                            .then_inc(stat_made, 1)

            batches(dve, body)


class Conditioning:
    pass


def conditioning(nc, m, own):
    (vec_turned, vec_ready, cond_turned, cond_ready, es_made, es_copied, es_turned, mod_step, mask_step,
     mask_out) = sems(own, nc, "co", "vec_turned", "vec_ready", "cond_turned", "cond_ready", "es_made",
                      "es_copied", "es_turned", "mod_step", "mask_step", "mask_out")
    VEC, ES_TURNED, ES, COND = 4, 5, 6, 7
    c = Conditioning()

    def tensor(pe, part):
        if part == 0:
            nc.tensor.transpose(m.bank[VEC][:, 0:VEC_ROWS], m.vec_rows[:, :], m.ident[0:VEC_ROWS, 0:VEC_ROWS])\
                .then_inc(vec_turned, 1)
            for k in range(KC):
                last = nc.tensor.transpose(m.bank[COND][:, k * B:(k + 1) * B], m.cond_rows[:, k * P:(k + 1) * P],
                                           m.ident[0:B, 0:B])
            last.then_inc(cond_turned, 1)
        elif part == 1:
            pe.wait_ge(cond_ready, 1)
            for k in range(KC):
                last = nc.tensor.matmul(m.bank[ES][0:B, :], m.condT[:, k, :], m.wc[:, k, :],
                                        start=(k == 0), stop=(k == KC - 1))
            last.then_inc(es_made, 1)
        elif part == 2:
            pe.wait_ge(es_copied, 1)
            for k in range(KC):
                last = nc.tensor.transpose(m.bank[ES_TURNED][:, k * B:(k + 1) * B],
                                           m.ss_rows[:, k * P:(k + 1) * P], m.ident[0:B, 0:B])
            last.then_inc(es_turned, 1)

    def scalar(act):
        act.wait_ge(cond_turned, 1)
        act.activation(m.condT[:, :, :], m.bank[COND][:, 0:KC * B].rearrange("p (k b) -> p k b", b=B), ACT.Silu)\
            .then_inc(cond_ready, 1)

    def vector(dve, part):
        if part == 0:
            dve.wait_ge(vec_turned, 1)
            dve.tensor_copy(m.vec[:, :], m.bank[VEC][:, 0:VEC_ROWS]).then_inc(vec_ready, 1)
            dve.tensor_scalar(m.mask_row[:, :], m.mask_row[:, :], -1.0, MASK_VALUE / MASK_UNIT, ALU.add, ALU.mult)\
                .then_inc(mask_step, 1)
            dve.wait_ge(mask_step, 1)
            dve.tensor_copy(m.mask_hi[:, :], m.mask_row[:, :]).then_inc(mask_step, 1)
            dve.wait_ge(mask_step, 2)
            dve.tensor_tensor(m.mask_lo[:, :], m.mask_row[:, :], m.mask_hi[:, :], ALU.subtract).then_inc(mask_step, 1)
        elif part == 2:
            dve.wait_ge(es_made, 1)
            dve.tensor_copy(m.ss_rows[:, :], m.bank[ES][0:B, :]).then_inc(es_copied, 1)
        elif part == 3:
            dve.wait_ge(es_turned, 1)
            dve.wait_ge(vec_ready, 1)
            es = m.bank[ES_TURNED][:, 0:KC * B].rearrange("p (k b) -> p k b", b=B)
            for k in range(KC):
                dve.tensor_scalar(m.mod1[:, k, :], es[:, k, :], m.vec[:, EMB_B + k:EMB_B + k + 1],
                                  1.0 if k < CT else 0.0, ALU.add, ALU.add).then_inc(mod_step, 1)
            dve.wait_ge(mod_step, KC)
            for h in range(CT):
                dve.tensor_scalar(m.mod1_scale[:, h, :], m.mod1[:, h, :], m.vec[:, SBN_W + h:SBN_W + h + 1], None,
                                  ALU.mult).then_inc(mod_step, 1)
                dve.scalar_tensor_tensor(m.mod1_shift[:, h, :], m.mod1[:, h, :],
                                         m.vec[:, SBN_B + h:SBN_B + h + 1], m.mod1[:, CT + h, :],
                                         ALU.mult, ALU.add).then_inc(mod_step, 1)
            dve.wait_ge(mod_step, KC + 2 * CT)

    def sync(sp):
        sp.wait_ge(mask_step, 3)
        sp.dma_start(m.mask_dram[0], m.mask_hi[:, :]).then_inc(mask_out, 16)
        sp.dma_start(m.mask_dram[1], m.mask_lo[:, :]).then_inc(mask_out, 16)
        sp.wait_ge(mask_out, 32)

    c.tensor, c.scalar, c.vector, c.sync = tensor, scalar, vector, sync
    return c


def finish(nc, layer, m):
    w = m.wo1 if layer else m.wo
    with ExitStack() as own:
        (step, root, src_ready, turned, srcT_ready, y_made, y_added, stat_step, xb_added) = sems(
            own, nc, f"fi{layer}", "step", "root", "src_ready", "turned", "srcT_ready", "y_made", "y_added",
            "stat_step", "xb_added")
        y_out_done = sems(own, nc, f"fi{layer}", "y_out_done0", "y_out_done1")
        cond = None if layer else conditioning(nc, m, own)
        block = own.enter_context(nc.Block())
        src = m.XN if layer else m.O

        @block.gpsimd
        def _(pool):
            if layer:
                pool.tensor_tensor(m.X[:, :, :], m.X[:, :, :],
                                   m.ob_row[:, :].unsqueeze(1).broadcast_to([P, NT, C]), ALU.add)\
                    .then_inc(xb_added, 1)

        @block.vector
        def _(dve):
            if layer:
                for t in range(NT):
                    dve.bn_aggr(m.moments[:, t, :], m.stats[:, t, :]).then_inc(stat_step, 1)
                dve.wait_ge(stat_step, NT)
                normalise(dve, None, m, step, root, True)
                for t in range(NT):
                    normal_tile(dve, m, m.O, t, True).then_inc(src_ready, 1)
                dve.wait_ge(xb_added, 1)
            for t in range(NT):
                if not layer and t % TPB == 0:
                    cond.vector(dve, t // TPB)
                dve.wait_ge(y_made, t + 1)
                if layer:
                    if t >= 2:
                        dve.wait_ge(y_out_done[t % 2], 16 * (t // 2))
                    dst = m.y_out[t % 2][:, :]
                else:
                    dst = m.X[:, t, :]
                dve.tensor_tensor(dst, m.bank[2 + t % 2][:, 0:C], m.X[:, t, :], ALU.add).then_inc(y_added, 1)
                if not layer:
                    dve.wait_ge(y_added, t + 1)
                    dve.bn_stats(m.stats[:, t, :], m.X[:, t, :]).then_inc(stat_step, 1)
            if not layer:
                dve.wait_ge(stat_step, NT)
                for t in range(NT):
                    dve.bn_aggr(m.moments[:, t, :], m.stats[:, t, :]).then_inc(stat_step, 1)
                dve.wait_ge(stat_step, 2 * NT)

        @block.scalar
        def _(act):
            if layer:
                normalise(None, act, m, step, root, True)
            else:
                cond.scalar(act)
            for b in range(B):
                for h in range(CT):
                    act.wait_ge(turned, CT * b + h + 1)
                    if b >= 2:
                        act.wait_ge(y_made, TPB * (b - 1))
                    if layer:
                        ins = act.activation(m.xT[b % 2][:, h, :], m.bank[h], ACT.Silu,
                                             bias=m.mod1_shift[:, h, b:b + 1], scale=m.mod1_scale[:, h, b:b + 1])
                    else:
                        ins = act.activation(m.xT[b % 2][:, h, :], m.bank[h], ACT.Copy)
                    ins.then_inc(srcT_ready, 1)

        @block.tensor
        def _(pe):
            def turn(b):
                for h in range(CT):
                    if b:
                        pe.wait_ge(srcT_ready, CT * (b - 1) + h + 1)
                    for t in range(TPB):
                        if layer:
                            pe.wait_ge(src_ready, TPB * b + t + 1)
                        last = nc.tensor.transpose(m.bank[h][:, t * P:(t + 1) * P],
                                                   src[:, TPB * b + t, h * P:(h + 1) * P], m.ident[:, :])
                    last.then_inc(turned, 1)

            if not layer:
                cond.tensor(pe, 0)
            turn(0)
            for b in range(B):
                if b + 1 < B:
                    turn(b + 1)
                if not layer and b:
                    cond.tensor(pe, b)
                pe.wait_ge(srcT_ready, CT * (b + 1))
                for t in range(TPB):
                    n = TPB * b + t
                    if n >= 2:
                        pe.wait_ge(y_added, n - 1)
                    for k in range(CT):
                        last = nc.tensor.matmul(m.bank[2 + n % 2][:, 0:C], m.xT[b % 2][:, k, t * P:(t + 1) * P],
                                                w[:, k, :], start=(k == 0), stop=(k == CT - 1))
                    last.then_inc(y_made, 1)

        @block.sync
        def _(sp):
            if not layer:
                cond.sync(sp)
            if layer:
                for t in range(NT):
                    b, q = divmod(t, TPB)
                    sp.wait_ge(y_added, t + 1)
                    sp.dma_start(m.out[b, q * P:(q + 1) * P, :], m.y_out[t % 2][:, :])\
                        .then_inc(y_out_done[t % 2], 16)
                for done in y_out_done:
                    sp.wait_ge(done, 16 * NT // 2)


_INS = ["x", "cond_2048", "mask_BxS_ff1", "L0_cond_pos", "L0_cond_rms_w", "L0_cond_w_cond", "L0_cond_w_qkv", "L0_cond_w_out",
        "L1_cond_norm_w", "L1_cond_norm_b", "L1_cond_q_w", "L1_cond_q_b", "L1_cond_k_w", "L1_cond_k_b",
        "L1_cond_v_w", "L1_cond_v_b", "L1_cond_emb_w", "L1_cond_emb_b", "L1_cond_sb_norm_w",
        "L1_cond_sb_norm_b", "L1_cond_out_w", "L1_cond_out_b"]


def kernel(**inputs):
    import numpy as np
    import concourse.bacc as bacc
    from concourse.bass_utils import run_bass_kernel_spmd

    nc = bacc.Bacc("TRN2", target_bir_lowering=False, num_devices=1)
    arrays, args = {}, []
    for name in _INS:
        a = np.ascontiguousarray(inputs[name])
        arrays[f"in_{name}"] = a
        args.append(nc.dram_tensor(f"in_{name}", a.shape, mybir.dt.from_np(a.dtype), kind="ExternalInput").ap())
    args.append(nc.dram_tensor("y", (B, S, C), F32, kind="ExternalOutput").ap())
    build(nc, *args)
    r = run_bass_kernel_spmd(nc, [arrays], core_ids=[0])
    return r.results[0]["y"]
```

```python
from contextlib import ExitStack

import concourse.bass as bass
from concourse import mybir

F32 = mybir.dt.float32
F16 = mybir.dt.float16
ALU = mybir.AluOpType
ACT = mybir.ActivationFunctionType
AX = mybir.AxisListType

P = 128
B, S, C, H = 4, 512, 256, 16
DH = C // H
TPB = S // P
NT = B * TPB
CT = C // P
COND = 2 * C
KC = COND // P
G = 4
NG = H // G
W32 = 32
QT = TPB
KT = TPB
EXPS = KT * G
MAXES = G * QT
LEAD = 2

EARLY = NT - TPB
FIRST = TPB

HIGH_LOW = [(0, 0), (0, 1), (1, 0), (1, 1)]
ROW_MASK = 4 * DH
ROW_SHIFT = 96
UNIT = 64.0
MASK_VALUE = 1e6

NORM_W, NORM_B, Q_B, K_B, SBN_W, SBN_B, EMB_B, MASK = 0, 2, 4, 6, 8, 10, 12, 16
VEC_ROWS = MASK + NT


class Buffers:
    pass


class RunAhead:
    pass


def build(nc, x, cond, mask, pos, rms_w, w_cond, w_qkv, w_out, norm_w, norm_b, q_w, q_b, k_w, k_b,
          v_w, v_b, emb_w, emb_b, sbn_w, sbn_b, out_w, out_b, out):
    m = Buffers()
    m.x, m.cond, m.mask, m.pos, m.out = x, cond, mask, pos, out
    m.rms_w, m.w_cond, m.w_qkv, m.w_out = rms_w, w_cond, w_qkv, w_out
    m.norm_w, m.norm_b, m.q_w, m.q_b, m.k_w, m.k_b, m.v_w, m.v_b = norm_w, norm_b, q_w, q_b, k_w, k_b, v_w, v_b
    m.emb_w, m.emb_b, m.sbn_w, m.sbn_b, m.out_w, m.out_b = emb_w, emb_b, sbn_w, sbn_b, out_w, out_b
    with ExitStack() as ctx:
        def sb(name, shape, dt=F32):
            return ctx.enter_context(nc.sbuf_tensor(name, shape, dt))

        m.bank = [ctx.enter_context(nc.psum_tensor(f"bank{i}", [P, 512], F32))[:, :] for i in range(8)]
        m.score_banks, m.max_banks, m.ACC, m.TURN = m.bank[0:2], m.bank[2:6], m.bank[6], m.bank[7]

        m.X = sb("X", [P, NT, C])
        m.V = sb("V", [P, NT, C])
        m.O = sb("O", [P, NT, C])
        m.XN = m.O
        m.xT = [sb(f"xT{i}", [P, CT, 512]) for i in range(2)]
        m.parts = [sb(f"parts{i}", [P, 2, 2 * CT, 512], F16) for i in range(2)]
        m.q_aug = [sb(f"q_aug{g}", [P, G, 512], F16) for g in range(NG)]
        m.k_aug = [sb(f"k_aug{g}", [P, G, 512], F16) for g in range(NG)]
        m.v_aug = [sb(f"v_aug{g}", [P, KT, G, W32]) for g in range(NG)]
        m.probs = [sb(f"probs{i}", [P, G, 512]) for i in range(KT)]
        m.oT = sb("oT", [P, 512])
        m.row_max = [sb(f"row_max{i}", [P, MAXES]) for i in range(2)]
        m.neg_max = [sb(f"neg_max{i}", [P, 2 * MAXES], F16) for i in range(2)]
        m.shift_rows = [sb(f"shift_rows{g}", [2 * MAXES, P], F16) for g in range(NG)]
        m.inv_sum = sb("inv_sum", [P, QT, G, 1])

        m.wqkv = sb("wqkv", [P, CT, 3 * C])
        m.wo = sb("wo", [P, CT, C])
        m.wqkv1 = sb("wqkv1", [P, CT, 3 * C])
        m.wo1 = sb("wo1", [P, CT, C])
        m.wc = sb("wc", [P, KC, COND])
        m.vb_row = sb("vb_row", [P, C])
        m.ob_row = sb("ob_row", [P, C])
        m.ident = sb("ident", [P, P])
        m.ident16 = sb("ident16", [P, P], F16)
        m.vec_rows = sb("vec_rows", [VEC_ROWS, P])
        m.vec = sb("vec", [P, VEC_ROWS])
        m.rms_rows = sb("rms_rows", [CT, P])
        m.rms_vec = sb("rms_vec", [P, CT])
        m.ss_rows = sb("ss_rows", [B, COND])
        m.cond_rows = sb("cond_rows", [B, COND])
        m.condT = sb("condT", [P, KC, B])
        m.mod0_scale = sb("mod0_scale", [P, CT, B])
        m.mod0_shift = sb("mod0_shift", [P, CT, B])
        m.es = sb("es", [P, KC, B])
        m.mod1 = sb("mod1", [P, KC, B])
        m.mod1_scale = sb("mod1_scale", [P, CT, B])
        m.mod1_shift = sb("mod1_shift", [P, CT, B])
        m.mask_row = sb("mask_row", [B, S])
        m.mask_hi = sb("mask_hi", [B, S], F16)
        m.mask_lo = sb("mask_lo", [B, S], F16)
        m.spare = sb("spare", [P, 1])
        m.stats = sb("stats", [P, NT, 6])
        m.moments = sb("moments", [P, NT, 2])
        m.spread = sb("spread", [P, NT])
        m.rstd = sb("rstd", [P, NT])
        m.mean_rstd = sb("mean_rstd", [P, FIRST])
        m.pos_rows = sb("pos_rows", [P, TPB, 2 * DH])
        m.sinT = sb("sinT", [P, S])
        m.cosT = sb("cosT", [P, S])
        m.rotate = sb("rotate", [P, P])
        m.plain, m.with_cos = ([m.probs[0][:, 2 * j + i, :] for i in range(2)] for j in range(2))
        m.roped = [m.probs[1][:, i, :] for i in range(2)]
        m.pos_wide = [m.probs[2][:, i, :] for i in range(2)]
        m.zeros = m.probs[3][:, 0:2, :].bitcast(F16).rearrange("p a (b n) -> p (a b) n", b=2)
        m.aug_fill = sb("aug_fill", [P, 2])
        m.v_tmp = [sb(f"v_tmp{i}", [P, C]) for i in range(2)]

        m.qk_dram = nc.dram_tensor("qk_parts", [B, 2, 2, C, S], F16, kind="Internal").ap()
        m.mask_dram = nc.dram_tensor("mask_parts", [2, B, S], F16, kind="Internal").ap()

        for layer in range(2):
            with ExitStack() as shared:
                ahead = RunAhead()
                (ahead.row_scores_made, ahead.max_made, ahead.shift_made, ahead.shift_turned, ahead.shift_copied,
                 ahead.shift_high_made, ahead.v_in) = sems(
                    shared, nc, f"ra{layer}", "row_scores_made", "max_made", "shift_made", "shift_turned",
                    "shift_copied", "shift_high_made", "v_in")
                ahead.operands_in = sems(shared, nc, f"ra{layer}", *[f"operands_in{g}" for g in range(NG)])
                ahead.parts_out = sems(shared, nc, f"ra{layer}", "parts_out0", "parts_out1")
                ahead.shift_in = sems(shared, nc, f"ra{layer}", *[f"shift_in{g}" for g in range(NG)])
                project(nc, layer, m, ahead)
                attend(nc, layer, m, ahead)
            finish(nc, layer, m)


def sems(ctx, nc, tag, *names):
    return [ctx.enter_context(nc.semaphore(f"{tag}_{n}")) for n in names]


def condition(nc, m, bank):
    for k in range(KC):
        last = nc.tensor.matmul(bank[0:B, :], m.condT[:, k, :], m.wc[:, k, :], start=(k == 0), stop=(k == KC - 1))
    return last


def turn_condition(nc, m, bank):
    for k in range(KC):
        last = nc.tensor.transpose(bank[:, k * B:(k + 1) * B], m.ss_rows[:, k * P:(k + 1) * P], m.ident[0:B, 0:B])
    return last


class Opening:
    pass


def opening(nc, m, own, step, root, xn_ready):
    (cond_in, wc_in, rms_in, rms_ready, pos_in, wqkv_in, late_in, ident_made, fill_made, rotate_made, ones_made,
     zeros_made, aug_made, cond_turned, cond_ready, ss_made, ss_copied, ss_turned, rms_turned, mod_made, stat_step,
     pos_wide_made, pos_turned, pos_copied) = sems(
        own, nc, "op", "cond_in", "wc_in", "rms_in", "rms_ready", "pos_in", "wqkv_in", "late_in", "ident_made",
        "fill_made", "rotate_made", "ones_made", "zeros_made", "aug_made", "cond_turned", "cond_ready", "ss_made",
        "ss_copied", "ss_turned", "rms_turned", "mod_made", "stat_step", "pos_wide_made", "pos_turned", "pos_copied")
    x_in = sems(own, nc, "op", *[f"x_in{b}" for b in range(B)])
    POS_BANKS, RMS, SS_TURNED, SS, COND = (4, 5), 3, 2, 6, 7
    rows = [(NORM_W, m.norm_w), (NORM_B, m.norm_b), (Q_B, m.q_b), (K_B, m.k_b),
            (SBN_W, m.sbn_w), (SBN_B, m.sbn_b), (EMB_B, m.emb_b)]
    def load_x(engine, b):
        engine.dma_start(m.X[:, b * TPB:(b + 1) * TPB, :], m.x[b].rearrange("(t p) c -> p t c", p=P))\
            .then_inc(x_in[b], 16)

    def sync(sp):
        sp.dma_start(m.cond_rows[:, :], m.cond).then_inc(cond_in, 16)
        sp.dma_start(m.rms_rows[:, :], m.rms_w.rearrange("(a p) -> a p", p=P)).then_inc(rms_in, 16)
        sp.dma_start(m.pos_rows[:, :, :], m.pos.rearrange("(t p) o d -> p t (o d)", p=P)).then_inc(pos_in, 16)
        for b in range(1, B):
            load_x(sp, b)
        for i, w in enumerate((m.q_w, m.k_w, m.v_w)):
            sp.dma_start(m.wqkv1[:, :, i * C:(i + 1) * C], w.rearrange("(k p) n -> p k n", p=P))\
                .then_inc(late_in, 16)
        for to, w in ((m.wo, m.w_out), (m.wo1, m.out_w)):
            sp.dma_start(to[:, :, :], w.rearrange("(k p) n -> p k n", p=P)).then_inc(late_in, 16)
        for to, v in ((m.vb_row, m.v_b), (m.ob_row, m.out_b)):
            sp.dma_start(to[:, :], v.partition_broadcast(P)).then_inc(late_in, 16)
        for at, v in rows:
            n = v.shape[0] // P
            sp.dma_start(m.vec_rows[at:at + n, :], v.rearrange("(a p) -> a p", p=P)).then_inc(late_in, 16)
        sp.dma_start(m.vec_rows[MASK:MASK + NT, :], m.mask.rearrange("b (t p) -> (b t) p", p=P))\
            .then_inc(late_in, 16)
        sp.dma_start(m.mask_row[:, :], m.mask).then_inc(late_in, 16)
        sp.wait_ge(ss_made, 1)
        sp.dma_start(m.wc[:, :, :], m.emb_w.rearrange("(k p) n -> p k n", p=P)).then_inc(late_in, 16)

    def sync_end(sp):
        sp.wait_ge(late_in, 16 * (7 + len(rows) + 3))

    def scalar(act):
        act.dma_start(m.wc[:, :, :], m.w_cond.rearrange("(k p) n -> p k n", p=P)).then_inc(wc_in, 16)
        load_x(act, 0)
        act.dma_start(m.wqkv[:, :, :], m.w_qkv.rearrange("(k p) n -> p k n", p=P)).then_inc(wqkv_in, 16)
        normalise(None, act, m, step, root, False, 0, 0, TPB)
        act.wait_ge(mod_made, CT + 1)

    def scalar_pos(act):
        act.wait_ge(pos_turned, 1)
        for to, bank in ((m.sinT, POS_BANKS[0]), (m.cosT, POS_BANKS[1])):
            act.activation(to[:, :], m.bank[bank], ACT.Copy).then_inc(pos_copied, 1)

    def scalar_rest(act):
        normalise(None, act, m, step, root, False, 1, TPB, NT)

    def gpsimd(pool):
        pool.memset(m.ident[:, :], 0.0).then_inc(ident_made, 1)
        pool.memset(m.ident16[:, :], 0.0).then_inc(ident_made, 1)
        pool.memset(m.rotate[:, :], 0.0).then_inc(rotate_made, 1)
        pool.memset(m.aug_fill[:, :], 0.0).then_inc(fill_made, 1)
        for n, t in enumerate((m.ident, m.ident16)):
            pool.wait_ge(ident_made, 2 + n)
            pool.affine_select(out=t[:, :], in_=t[:, :], compare_op=ALU.not_equal, fill=1.0, base=0,
                               pattern=[[-1, P]], channel_multiplier=1).then_inc(ident_made, 1)
        for n, (col, row, value) in enumerate([(0, ROW_MASK, UNIT), (0, ROW_MASK + 1, UNIT),
                                               (1, ROW_SHIFT, UNIT), (1, ROW_SHIFT + 1, UNIT)]):
            pool.wait_ge(fill_made, 1 + n)
            at = m.aug_fill[:, col:col + 1]
            pool.affine_select(out=at, in_=at, compare_op=ALU.not_equal, fill=value, base=-row,
                               pattern=[[0, 1]], channel_multiplier=1).then_inc(fill_made, 1)
        pool.wait_ge(rotate_made, 1)
        halves = m.rotate[:, :].rearrange("p (h two d) -> p h two d", two=2, d=DH // 2)
        for half, (base, value) in enumerate([(-DH // 2, -1.0), (0, 1.0)]):
            pool.affine_select(out=halves[:, :, half, :], in_=halves[:, :, half, :], compare_op=ALU.not_equal,
                               fill=value, base=base, pattern=[[-DH, P // DH], [-1, DH // 2]],
                               channel_multiplier=1).then_inc(rotate_made, 1)
        pool.wait_ge(pos_in, 16)
        both = m.pos_rows[:, :, :].rearrange("p t (d two) -> p t two d", two=2)
        for i in range(2):
            pool.tensor_copy(m.pos_wide[i].rearrange("p (t h d) -> p t h d", t=TPB, d=DH),
                             both[:, :, i:i + 1, :].broadcast_to([P, TPB, P // DH, DH])).then_inc(pos_wide_made, 1)
        for g in range(NG):
            pool.memset(m.v_aug[g][:, :, :, DH:W32], 0.0).then_inc(ones_made, 1)
        pool.wait_ge(ones_made, NG)
        for g in range(NG):
            pool.memset(m.v_aug[g][:, :, :, DH:DH + 1], 1.0).then_inc(ones_made, 1)
        pool.wait_ge(ones_made, 2 * NG)

    def tensor_cond(pe):
        pe.wait_ge(ident_made, 4)
        pe.wait_ge(cond_in, 16)
        for k in range(KC):
            last = nc.tensor.transpose(m.bank[COND][:, k * B:(k + 1) * B], m.cond_rows[:, k * P:(k + 1) * P],
                                       m.ident[0:B, 0:B])
        last.then_inc(cond_turned, 1)

    def tensor_product(pe):
        pe.wait_ge(cond_ready, 1)
        pe.wait_ge(wc_in, 16)
        condition(nc, m, m.bank[SS]).then_inc(ss_made, 1)

    def tensor_ss(pe):
        pe.wait_ge(ss_copied, 1)
        turn_condition(nc, m, m.bank[SS_TURNED]).then_inc(ss_turned, 1)

    def tensor_rms(pe):
        pe.wait_ge(rms_in, 16)
        nc.tensor.transpose(m.bank[RMS][:, 0:CT], m.rms_rows[:, :], m.ident[0:CT, 0:CT]).then_inc(rms_turned, 1)

    def tensor_pos(pe):
        pe.wait_ge(pos_wide_made, 2)
        for i in range(2):
            for t in range(TPB):
                last = nc.tensor.transpose(m.bank[POS_BANKS[i]][:, t * P:(t + 1) * P],
                                           m.pos_wide[i][:, t * P:(t + 1) * P], m.ident[:, :])
        last.then_inc(pos_turned, 1)

    def stats(dve, b):
        dve.wait_ge(x_in[b], 16)
        for t in range(TPB * b, TPB * (b + 1)):
            dve.bn_stats(m.stats[:, t, :], m.X[:, t, :]).then_inc(stat_step, 1)

    def vector(dve):
        dve.memset(m.zeros, 0.0).then_inc(zeros_made, 1)
        dve.wait_ge(cond_turned, 1)
        dve.tensor_copy(m.condT[:, :, :], m.bank[COND][:, 0:KC * B].rearrange("p (k b) -> p k b", b=B))\
            .then_inc(cond_ready, 1)
        stats(dve, 0)
        dve.wait_ge(stat_step, TPB)
        for t in range(TPB):
            dve.bn_aggr(m.moments[:, t, :], m.stats[:, t, :]).then_inc(stat_step, 1)
        dve.wait_ge(stat_step, 2 * TPB)
        normalise(dve, None, m, step, root, False, 0, 0, TPB)
        for t in range(TPB):
            normal_tile(dve, m, m.X, t, False).then_inc(xn_ready, 1)
        dve.wait_ge(rms_turned, 1)
        dve.tensor_copy(m.rms_vec[:, :], m.bank[RMS][:, 0:CT]).then_inc(rms_ready, 1)
        stats(dve, 1)
        dve.wait_ge(ss_made, 1)
        dve.tensor_copy(m.ss_rows[:, :], m.bank[SS][0:B, :]).then_inc(ss_copied, 1)
        dve.wait_ge(ss_turned, 1)
        dve.wait_ge(rms_ready, 1)
        ss = m.bank[SS_TURNED][:, 0:KC * B].rearrange("p (k b) -> p k b", b=B)
        for h in range(CT):
            dve.tensor_scalar(m.mod0_scale[:, h, :], ss[:, h, :], 1.0, m.rms_vec[:, h:h + 1],
                              ALU.add, ALU.mult).then_inc(mod_made, 1)
        dve.tensor_copy(m.mod0_shift[:, :, :], ss[:, CT:2 * CT, :]).then_inc(mod_made, 1)
        for b in range(2, B):
            stats(dve, b)
        done = 2 * TPB
        dve.wait_ge(stat_step, done + NT - TPB)
        for t in range(TPB, NT):
            dve.bn_aggr(m.moments[:, t, :], m.stats[:, t, :]).then_inc(stat_step, 1)
        dve.wait_ge(stat_step, 2 * NT)
        normalise(dve, None, m, step, root, False, 1, TPB, NT)

    def fill(dve, f):
        if f == 0:
            dve.wait_ge(zeros_made, 1)
            dve.wait_ge(fill_made, 5)
        g, side = divmod(f, 2)
        dve.tensor_scalar((m.q_aug, m.k_aug)[side][g][:, :, :], m.zeros, m.aug_fill[:, side:side + 1], None, ALU.add)\
           .then_inc(aug_made, 1)

    o = Opening()
    o.wqkv_in, o.rotate_made, o.pos_copied, o.aug_made = wqkv_in, rotate_made, pos_copied, aug_made
    o.sync, o.sync_end, o.gpsimd = sync, sync_end, gpsimd
    o.scalar, o.scalar_pos, o.scalar_rest = scalar, scalar_pos, scalar_rest
    o.tensor_cond, o.tensor_rms, o.tensor_product, o.tensor_ss, o.tensor_pos = (
        tensor_cond, tensor_rms, tensor_product, tensor_ss, tensor_pos)
    o.vector, o.fill = vector, fill
    return o


def normalise_begin(dve, m, step, centred, chain, t0, t1):
    spread, rstd, mean, var = m.spread[:, t0:t1], m.rstd[:, t0:t1], m.moments[:, t0:t1, 0], m.moments[:, t0:t1, 1]
    if centred:
        dve.tensor_scalar(spread, var, 1e-5, None, ALU.add).then_inc(step, 1)
    else:
        dve.tensor_tensor(rstd, mean, mean, ALU.mult).then_inc(step, 1)
        dve.wait_ge(step, 3 * chain + 1)
        dve.scalar_tensor_tensor(spread, var, 1e-6, rstd, ALU.add, ALU.add).then_inc(step, 1)


def normalise_end(dve, m, step, root, centred, chain, t0, t1):
    dve.wait_ge(root, chain + 1)
    dve.reciprocal(m.rstd[:, t0:t1], m.spread[:, t0:t1]).then_inc(step, 1)
    dve.wait_ge(step, (2 if centred else 3) * (chain + 1))


def normalise(dve, act, m, step, root, centred, chain=0, t0=0, t1=NT):
    if dve is not None:
        normalise_begin(dve, m, step, centred, chain, t0, t1)
        normalise_end(dve, m, step, root, centred, chain, t0, t1)
    if act is not None:
        act.wait_ge(step, (2 if centred else 3) * (chain + 1) - 1)
        act.activation(m.spread[:, t0:t1], m.spread[:, t0:t1], ACT.Sqrt).then_inc(root, 1)


def normal_tile(dve, m, src, t, centred):
    if centred:
        return dve.tensor_scalar(m.XN[:, t, :], src[:, t, :], m.moments[:, t, 0:1], m.rstd[:, t:t + 1],
                                 ALU.subtract, ALU.mult)
    return dve.tensor_scalar(m.XN[:, t, :], src[:, t, :], m.rstd[:, t:t + 1], None, ALU.mult)


def load_operands(sp, m, layer, b, g, done):
    for r, (qp, kp) in enumerate(HIGH_LOW):
        for aug, side, part in ((m.q_aug, 0, qp), (m.k_aug, 1, kp)):
            sp.dma_start(aug[g][r * DH:(r + 1) * DH, :, :],
                         m.qk_dram[b, side, part, g * G * DH:(g + 1) * G * DH, :]
                         .rearrange("(h d) t -> d h t", d=DH)).then_inc(done, 16)
    if layer:
        for part in range(2):
            row = ROW_MASK + part
            sp.dma_start(m.k_aug[g][row:row + 1, :, :],
                         m.mask_dram[part, bass.ds(b, 1), :].unsqueeze(1).broadcast_to([1, G, S])).then_inc(done, 16)


def loads_of(layer):
    return 2 * len(HIGH_LOW) + 2 * layer


def group_values(pool, m, b, g):
    return pool.tensor_copy(m.v_aug[g][:, :, :, 0:DH],
                            m.V[:, bass.ds(b * TPB, TPB), g * G * DH:(g + 1) * G * DH]
                            .rearrange("p t (h d) -> p t h d", d=DH))


def shift_high(dve, m, i):
    return dve.tensor_scalar(m.neg_max[i][:, 0:MAXES], m.row_max[i][:, :], -1.0 / UNIT, None, ALU.mult)


def shift_low(dve, m, i):
    return dve.scalar_tensor_tensor(m.neg_max[i][:, MAXES:2 * MAXES], m.row_max[i][:, :], -1.0 / UNIT,
                                    m.neg_max[i][:, 0:MAXES], ALU.mult, ALU.subtract)


def row_score_tile(nc, m, g, j, bank):
    h, q = divmod(j, QT)
    return nc.tensor.matmul(bank, m.q_aug[g][0:ROW_SHIFT, h, q * P:(q + 1) * P],
                            m.k_aug[g][0:ROW_SHIFT, h, :], start=True, stop=True)


def project(nc, layer, m, ahead):
    w = m.wqkv1 if layer else m.wqkv
    with ExitStack() as own:
        (step, root, xn_ready, x_turned, xT_ready, qk_made, plain_ready, rotated, sin_done, cos_done, rope_done,
         high_made, low_made, v_made, v_read, v_ready, aggregated, table_loaded) = sems(
            own, nc, f"pr{layer}", "step", "root", "xn_ready", "x_turned", "xT_ready", "qk_made", "plain_ready",
            "rotated", "sin_done", "cos_done", "rope_done", "high_made", "low_made", "v_made", "v_read",
            "v_ready", "aggregated", "table_loaded")
        start = None if layer else opening(nc, m, own, step, root, xn_ready)
        NQ = 2 * CT
        PRODUCTS = NQ + TPB
        ROWS = [(0, 0), (0, 2), (2, 1), (2, 1)]
        TURN_BANKS, QK_BANKS, V_BANKS, ROT_BANKS = (0, 1), (2, 3), (4, 5), (6, 7)
        SHIFT_AT = 1
        turn16 = m.bank[V_BANKS[0]].bitcast(F16)

        def rows_with(b, i):
            n = sum(NQ * ROWS[c][0] + TPB * ROWS[c][1] for c in range(b))
            n += min(i, NQ) * ROWS[b][0] + max(i - NQ, 0) * ROWS[b][1]
            return range(n, n + ROWS[b][i >= NQ])

        def part(n, hl):
            return m.parts[n // NQ % 2][:, hl, n % NQ, :]

        def bias(n):
            at = (Q_B if n % NQ < CT else K_B) + n % CT
            return m.vec[:, at:at + 1]

        def parts_free(engine, n):
            b = n // NQ
            if b >= 2 and n % NQ == 0:
                engine.wait_ge(ahead.parts_out[b % 2], 16 * NQ * (b // 2))

        block = own.enter_context(nc.Block())

        @block.vector
        def _(dve):
            def more_tokens(dve, first, tiles):
                for t in range(first, first + tiles):
                    normal_tile(dve, m, m.X, t, bool(layer)).then_inc(xn_ready, 1)

            def last_statistics():
                for t in range(EARLY, NT):
                    dve.bn_stats(m.stats[:, t, :], m.X[:, t, :]).then_inc(aggregated, 1)
                done = EARLY - FIRST + TPB
                dve.wait_ge(aggregated, done)
                for t in range(EARLY, NT):
                    dve.bn_aggr(m.moments[:, t, :], m.stats[:, t, :]).then_inc(aggregated, 1)
                dve.wait_ge(aggregated, done + TPB)
                normalise_begin(dve, m, step, True, 1, EARLY, NT)

            if layer:
                for t in range(FIRST, EARLY):
                    dve.bn_aggr(m.moments[:, t, :], m.stats[:, t, :]).then_inc(aggregated, 1)
                dve.wait_ge(aggregated, EARLY - FIRST)
                normalise(dve, None, m, step, root, True, 0, FIRST, EARLY)
                more_tokens(dve, FIRST, TPB)
            else:
                start.vector(dve)
                more_tokens(dve, TPB, TPB)
                dve.wait_ge(start.pos_copied, 2)

            def rope(n):
                f = m.roped[n % 2][:, :]
                dve.wait_ge(rotated, n + 1)
                if n >= 2:
                    dve.wait_ge(high_made, n - 1)
                    dve.wait_ge(low_made, n - 1)
                dve.tensor_tensor(f, m.bank[ROT_BANKS[n % 2]], m.sinT[:, :], ALU.mult).then_inc(sin_done, 1)
                dve.wait_ge(sin_done, n + 1)
                dve.wait_ge(cos_done, n + 1)
                dve.tensor_tensor(f, f, m.with_cos[n % 2][:, :], ALU.add).then_inc(rope_done, 1)

            def low(n):
                dve.wait_ge(high_made, n + 1)
                parts_free(dve, n)
                if layer:
                    ins = dve.scalar_tensor_tensor(part(n, 1), m.bank[QK_BANKS[n % 2]], bias(n), part(n, 0),
                                                   ALU.add, ALU.subtract)
                else:
                    ins = dve.tensor_tensor(part(n, 1), m.roped[n % 2][:, :], part(n, 0), ALU.subtract)
                ins.then_inc(low_made, 1)

            def v_bias(n):
                dve.wait_ge(v_made, n + 1)
                if n >= 2:
                    dve.wait_ge(v_ready, n - 1)
                dve.tensor_tensor(m.v_tmp[n % 2][:, :], m.bank[V_BANKS[n % 2]][:, 0:C], m.vb_row[:, :],
                                  ALU.add).then_inc(v_read, 1)

            def maximum(b, i, k):
                for n in rows_with(b, i)[k:k + 1]:
                    g, j = divmod(n, MAXES)
                    dve.wait_ge(ahead.row_scores_made, n + 1)
                    dve.tensor_reduce(m.row_max[g][:, j:j + 1], m.bank[TURN_BANKS[n % 2]], AX.X, ALU.max)\
                       .then_inc(ahead.max_made, 1)
                    if n == MAXES - 1:
                        dve.wait_ge(ahead.max_made, MAXES)
                        shift_high(dve, m, 0).then_inc(ahead.shift_high_made, 1)
                        dve.wait_ge(ahead.shift_high_made, 1)
                        shift_low(dve, m, 0).then_inc(ahead.shift_made, 1)

            for b in range(B):
                for i in range(NQ):
                    n = NQ * b + i
                    if layer and i:
                        low(n - 1)
                    maximum(b, i, 0)
                    maximum(b, i, 1)
                    if not layer and i > 1:
                        low(n - 2)
                    if not layer and i:
                        rope(n - 1)
                    if layer and b == 0 and i == 1:
                        last_statistics()
                    if layer and b == 0 and i == NQ - 1:
                        normalise_end(dve, m, step, root, True, 1, EARLY, NT)
                    if b == 0 and i == 2:
                        more_tokens(dve, 2 * TPB, TPB)
                    if not layer and b == 1:
                        start.fill(dve, TPB + i)
                n = NQ * b + NQ - 1
                if layer:
                    low(n)
                else:
                    rope(n)
                for t in range(TPB):
                    if t:
                        maximum(b, NQ + t - 1, 0)
                    if layer:
                        v_bias(TPB * b + t)
                    elif t in (1, 2):
                        low(n + t - 2)
                    if t:
                        maximum(b, NQ + t - 1, 1)
                    if b == 0:
                        more_tokens(dve, 3 * TPB + t, 1)
                    if not layer and b == 0:
                        start.fill(dve, t)
                for k in range(CT):
                    maximum(b, PRODUCTS - 1, k)
            dve.wait_ge(ahead.shift_made, 1)
            dve.wait_ge(ahead.max_made, LEAD * MAXES)

        @block.scalar
        def _(act):
            if not layer:
                start.scalar(act)

            def turn(b):
                for h in range(CT):
                    act.wait_ge(x_turned, CT * b + h + 1)
                    if b >= 2:
                        act.wait_ge(v_made, TPB * (b - 1))
                    tokens_in(act, m, layer, b, h).then_inc(xT_ready, 1)

            def plain(n):
                act.wait_ge(qk_made, n + 1)
                if n >= 2:
                    act.wait_ge(rotated, n - 1)
                    act.wait_ge(cos_done, n - 1)
                act.activation(m.plain[n % 2][:, :], m.bank[QK_BANKS[n % 2]], ACT.Copy,
                               scale=float(DH) ** -0.5 if n % NQ < CT else 1.0).then_inc(plain_ready, 1)

            def high(n):
                parts_free(act, n)
                if layer:
                    act.wait_ge(qk_made, n + 1)
                    ins = act.activation(part(n, 0), m.bank[QK_BANKS[n % 2]], ACT.Identity, bias=bias(n))
                else:
                    act.wait_ge(rope_done, n + 1)
                    ins = act.activation(part(n, 0), m.roped[n % 2][:, :], ACT.Copy)
                ins.then_inc(high_made, 1)

            if layer:
                act.sem_inc(x_turned, CT)
                act.sem_inc(xT_ready, CT)
                normalise(None, act, m, step, root, True, 0, FIRST, EARLY)
            else:
                turn(0)
                start.scalar_pos(act)
            for b in range(B):
                for i in range(NQ):
                    n = NQ * b + i
                    if layer:
                        high(n)
                        if n == 2:
                            normalise(None, act, m, step, root, True, 1, EARLY, NT)
                    else:
                        plain(n)
                        if n == 1:
                            start.scalar_rest(act)
                        if i:
                            high(n - 1)
                    if b == B - 1 and i == SHIFT_AT:
                        act.wait_ge(ahead.shift_turned, 1)
                        act.activation(m.shift_rows[0][:, :], turn16[0:2 * MAXES, 0:P], ACT.Copy)\
                            .then_inc(ahead.shift_copied, 1)
                for t in range(TPB):
                    n = TPB * b + t
                    if not layer:
                        act.wait_ge(v_made, n + 1)
                        act.activation(m.V[:, n, :], m.bank[V_BANKS[t % 2]][:, 0:C], ACT.Copy).then_inc(v_read, 1)
                        if t == 1:
                            high(NQ * b + NQ - 1)
                    if t == 0 and b + 1 < B:
                        turn(b + 1)
                    if layer:
                        act.wait_ge(v_read, n + 1)
                        act.activation(m.V[:, n, :], m.v_tmp[n % 2][:, :], ACT.Copy,
                                       scale=m.vec[:, MASK + n:MASK + n + 1]).then_inc(v_ready, 1)
                    if t == 1 and b == B - 1:
                        act.activation(m.spare[:, :], m.ident[:, 0:1], ACT.Exp).then_inc(table_loaded, 1)
            act.wait_ge(table_loaded, 1)

        @block.gpsimd
        def _(pool):
            if not layer:
                start.gpsimd(pool)
                pool.wait_ge(start.pos_copied, 2)
            if layer:
                pool.wait_ge(v_ready, TPB)
                for g in range(NG):
                    group_values(pool, m, 0, g).then_inc(ahead.v_in, 1)
            else:
                for n in range(NQ * B):
                    pool.wait_ge(plain_ready, n + 1)
                    if n >= 2:
                        pool.wait_ge(rope_done, n - 1)
                    pool.tensor_tensor(m.with_cos[n % 2][:, :], m.plain[n % 2][:, :], m.cosT[:, :], ALU.mult)\
                        .then_inc(cos_done, 1)
                    if NQ < n <= NQ + NG:
                        pool.wait_ge(v_read, TPB)
                        group_values(pool, m, 0, n - NQ - 1).then_inc(ahead.v_in, 1)
            pool.wait_ge(ahead.v_in, NG)

        @block.tensor
        def _(pe):
            def turn(b):
                for h in range(CT):
                    if b:
                        pe.wait_ge(xT_ready, CT * (b - 1) + h + 1)
                    if b and rows_with(b - 1, NQ).start:
                        pe.wait_ge(ahead.max_made, rows_with(b - 1, NQ).start - 1 + h)
                    for t in range(TPB):
                        if not layer:
                            pe.wait_ge(xn_ready, TPB * b + t + 1)
                        elif TPB * b + t >= FIRST:
                            pe.wait_ge(xn_ready, TPB * b + t - FIRST + 1)
                        last = nc.tensor.transpose(m.bank[h][:, t * P:(t + 1) * P],
                                                   m.XN[:, TPB * b + t, h * P:(h + 1) * P], m.ident[:, :])
                    last.then_inc(x_turned, 1)

            def row_scores(product, k):
                b, i = product
                for n in rows_with(b, i)[k:k + 1]:
                    g, j = divmod(n, MAXES)
                    if j == 0:
                        pe.wait_ge(ahead.operands_in[g], 16 * loads_of(layer))
                    if i >= NQ and b + 1 < B:
                        pe.wait_ge(xT_ready, CT * (b + 2))
                    if n >= 2:
                        pe.wait_ge(ahead.max_made, n - 1)
                    row_score_tile(nc, m, g, j, m.bank[TURN_BANKS[n % 2]]).then_inc(ahead.row_scores_made, 1)

            def queries_keys(n, rows):
                if n >= 2:
                    pe.wait_ge(low_made if layer else plain_ready, n - 1)
                i = n % NQ
                for k in range(CT):
                    if i == 0:
                        pe.wait_ge(xT_ready, CT * (n // NQ) + k + 1)
                    last = nc.tensor.matmul(m.bank[QK_BANKS[n % 2]], w[:, k, i * P:(i + 1) * P],
                                            m.xT[n // NQ % 2][:, k, :], start=(k == 0), stop=(k == CT - 1))
                    if k == CT - 1:
                        last.then_inc(qk_made, 1)
                    row_scores(rows, k)

            def rotate(n):
                pe.wait_ge(plain_ready, n + 1)
                if n >= 2:
                    pe.wait_ge(sin_done, n - 1)
                nc.tensor.matmul(m.bank[ROT_BANKS[n % 2]], m.rotate[:, :], m.plain[n % 2][:, :],
                                 start=True, stop=True).then_inc(rotated, 1)

            if not layer:
                start.tensor_cond(pe)
                start.tensor_rms(pe)
                start.tensor_product(pe)
                turn(0)
                start.tensor_ss(pe)
                start.tensor_pos(pe)
                pe.wait_ge(start.wqkv_in, 16)
                pe.wait_ge(start.rotate_made, 3)
            for b in range(B):
                for i in range(NQ):
                    queries_keys(NQ * b + i, (b, i))
                    if i and not layer:
                        rotate(NQ * b + i - 1)
                    if b == B - 1 and i == SHIFT_AT:
                        pe.wait_ge(ahead.shift_made, 1)
                        pe.wait_ge(v_read, TPB * b - 1)
                        nc.tensor.transpose(turn16[0:2 * MAXES, 0:P], m.neg_max[0][:, :], m.ident16[:, :])\
                            .then_inc(ahead.shift_turned, 1)
                if not layer:
                    rotate(NQ * b + NQ - 1)
                for t in range(TPB):
                    n = TPB * b + t
                    if n >= 2:
                        pe.wait_ge(v_read, n - 1)
                    elif not layer:
                        pe.wait_ge(start.pos_copied, 2)
                    if n == TPB * (B - 1):
                        pe.wait_ge(ahead.shift_copied, 1)
                    for k in range(CT):
                        last = nc.tensor.matmul(m.bank[V_BANKS[n % 2]][:, 0:C], m.xT[b % 2][:, k, t * P:(t + 1) * P],
                                                w[:, k, 2 * C:3 * C], start=(k == 0), stop=(k == CT - 1))
                        if k == CT - 1:
                            last.then_inc(v_made, 1)
                        if t:
                            row_scores((b, NQ + t - 1), k)
                    if t == 0 and b + 1 < B:
                        turn(b + 1)
                for k in range(CT):
                    row_scores((b, PRODUCTS - 1), k)

        @block.sync
        def _(sp):
            if not layer:
                start.sync(sp)
            for n in range(NQ * B):
                b, i = divmod(n, NQ)
                if (b, i) == (B - 1, SHIFT_AT + 1):
                    sp.wait_ge(ahead.shift_copied, 1)
                    sp.dma_start(m.q_aug[0][ROW_SHIFT:ROW_SHIFT + 2, :, :], m.shift_rows[0][:, :])\
                        .then_inc(ahead.shift_in[0], 16)
                sp.wait_ge(low_made, n + 1)
                sp.dma_start(m.qk_dram[b, i // CT, :, (i % CT) * P:(i % CT + 1) * P, :]
                             .rearrange("l p t -> p l t"), m.parts[b % 2][:, :, i, :])\
                    .then_inc(ahead.parts_out[b % 2], 16)
                if NQ - 1 <= n < NQ - 1 + NG:
                    g = n - NQ + 1
                    if g == 0:
                        sp.wait_ge(ahead.parts_out[0], 16 * NQ)
                    if not layer:
                        sp.wait_ge(start.aug_made, 2 * (g + 1))
                    load_operands(sp, m, layer, 0, g, ahead.operands_in[g])
            sp.wait_ge(ahead.shift_in[0], 16)
            for loaded in ahead.operands_in:
                sp.wait_ge(loaded, 16 * loads_of(layer))
            if not layer:
                start.sync_end(sp)


def attend(nc, layer, m, ahead):
    LOADS = loads_of(layer)
    with ExitStack() as own:
        (scores_made, exp_made, probs_used, acc_copied, o_turned, o_written, inv_made, stat_step, rstd_step, root,
         tokens_ready, turned, tokens_copied, bias_added) = sems(
            own, nc, f"at{layer}", "scores_made", "exp_made", "probs_used", "acc_copied", "o_turned",
            "o_written", "inv_made", "stat_step", "rstd_step", "root",
            "tokens_ready", "turned", "tokens_copied", "bias_added")
        block = own.enter_context(nc.Block())
        turn16 = m.TURN.bitcast(F16)

        def after(b, g, groups):
            return b + (g + groups) // NG, (g + groups) % NG

        def score_bank(h, wide):
            return m.bank[h if wide else h % 2]

        def before(b, g):
            return (b, g - 1) if g else (b - 1, NG - 1)

        def groups(engine, step):
            step(0, 0, True, False)
            with engine.Fori(0, B - 1) as b:
                for g in range(1, NG):
                    step(b, g, False, False)
                step(b + 1, 0, False, False)
            for g in range(1, NG):
                step(B - 1, g, False, True)

        def batches(engine, body):
            with engine.Fori(0, B - 1) as b:
                body(b, False)
            body(B - 1, True)

        @block.sync
        def _(sp):
            for out in ahead.parts_out:
                sp.wait_ge(out, 16 * 2 * CT * B // 2)

            def shift(b, g):
                sp.wait_ge(ahead.shift_copied, b * NG + g + 1)
                sp.dma_start(m.q_aug[g][ROW_SHIFT:ROW_SHIFT + 2, :, :], m.shift_rows[g][:, :])\
                    .then_inc(ahead.shift_in[g], 16)

            def body(b, last):
                for g in range(NG):
                    s = b * NG + g
                    if not (last and g == NG - 1):
                        shift(*after(b, g, 1))
                    if not last:
                        sp.wait_ge(scores_made, EXPS * (s + 1))
                        load_operands(sp, m, layer, b + 1, g, ahead.operands_in[g])

            batches(sp, body)

        @block.gpsimd
        def _(pool):
            def body(b, last):
                if last:
                    if layer:
                        pool.tensor_tensor(m.X[:, :, :], m.X[:, :, :],
                                           m.ob_row[:, :].unsqueeze(1).broadcast_to([P, NT, C]), ALU.add)\
                            .then_inc(bias_added, 1)
                        pool.wait_ge(bias_added, 1)
                    return
                for g in range(NG):
                    s = b * NG + g
                    pool.wait_ge(probs_used, KT + KT * (s + 1))
                    group_values(pool, m, b + 1, g).then_inc(ahead.v_in, 1)

            batches(pool, body)

        @block.tensor
        def _(pe):
            def row_scores(b, g, j):
                if j == 0:
                    pe.wait_ge(ahead.operands_in[g], 16 * LOADS * (b + 1))
                pe.wait_ge(ahead.max_made, MAXES * (b * NG + g) + j - 3)
                row_score_tile(nc, m, g, j, m.max_banks[j % 4]).then_inc(ahead.row_scores_made, 1)

            def turn_shift(s, g, turned):
                pe.wait_ge(ahead.shift_made, s + 1)
                pe.wait_ge(o_written, 1 + turned)
                nc.tensor.transpose(turn16[0:2 * MAXES, 0:P], m.neg_max[g % 2][:, :], m.ident16[:, :])\
                    .then_inc(ahead.shift_turned, 1)

            def scores(b, g, k, h, wide):
                if k == 0 and h == 0:
                    pe.wait_ge(ahead.shift_in[g], 16 * (b + 1))
                pe.wait_ge(exp_made, EXPS * (b * NG + g) + G * k + h + (1 if k == 0 or not wide else -1))
                if wide and k == 0 and h == 2:
                    pe.wait_ge(ahead.max_made, MAXES * NG * B)
                nc.tensor.matmul(score_bank(h, wide), m.k_aug[g][0:ROW_SHIFT + 2, h, k * P:(k + 1) * P],
                                 m.q_aug[g][0:ROW_SHIFT + 2, h, :], start=True, stop=True)\
                    .then_inc(scores_made, 1)

            def values(s, g, k, half):
                if k == 0 and half == 0:
                    pe.wait_ge(ahead.v_in, s + 1)
                    pe.wait_ge(acc_copied, 1 + s)
                pe.wait_ge(exp_made, 2 + EXPS * s + G * (k + 1))
                at = slice(half * S // 2, (half + 1) * S // 2)
                for h in range(G):
                    last = nc.tensor.matmul(m.ACC[W32 * h:W32 * (h + 1), at], m.v_aug[g][:, k, h, :],
                                            m.probs[k][:, h, at], start=(k == 0 and half == 0), stop=(k == KT - 1),
                                            tile_position=(0, W32 * h), skip_group_check=True)
                if half == 1:
                    last.then_inc(probs_used, 1)

            def turn_output(s, shifts):
                pe.wait_ge(acc_copied, 1 + s + 1)
                pe.wait_ge(ahead.shift_copied, shifts)
                pe.wait_ge(o_written, 1 + s)
                for q in range(QT):
                    last = nc.tensor.transpose(m.TURN[:, q * P:(q + 1) * P], m.oT[:, q * P:(q + 1) * P],
                                               m.ident[:, :])
                last.then_inc(o_turned, 1)

            def step(b, g, first, last):
                s = b * NG + g
                more = not (last and g >= NG - LEAD)
                final = last and g == NG - 1
                for k in range(KT):
                    for h in range(G):
                        scores(b, g, k, h, not more)
                        if more:
                            row_scores(*after(b, g, LEAD), G * k + h)
                        if h % 2 and k > 0:
                            values(s, g, k - 1, h // 2)
                        if h % 2 and k == 0 and not first:
                            values(s - 1, (g - 1) % NG, KT - 1, h // 2)
                    if k == 1 and not final:
                        turn_shift(s + 1, (g + 1) % NG, 0 if first else s - 1)
                    if k == 2 and not first:
                        turn_output(s - 1, s + (1 if final else 2))
                if final:
                    for half in range(2):
                        values(s, g, KT - 1, half)
                    if layer:
                        turn_output(s, B * NG)
                    pe.wait_ge(exp_made, 2 + EXPS * NG * B)
                    if layer:
                        pe.wait_ge(tokens_ready, TPB)
                    turn_batch(nc, m, m.O, 0, turned)
                    if not layer:
                        turn_output(s, B * NG)

            groups(pe, step)

        @block.scalar
        def _(act):
            act.sem_inc(exp_made, 2)
            act.sem_inc(probs_used, KT)
            act.sem_inc(acc_copied, 1)
            act.sem_inc(o_turned, 1)
            act.sem_inc(o_written, 1)

            def copy_shift(b, g):
                act.wait_ge(ahead.shift_turned, b * NG + g + 1)
                act.activation(m.shift_rows[g][:, :], turn16[0:2 * MAXES, 0:P], ACT.Copy)\
                    .then_inc(ahead.shift_copied, 1)

            def copy_output(s):
                act.wait_ge(probs_used, KT + KT * (s + 1))
                act.wait_ge(o_turned, 1 + s)
                act.activation(m.oT[:, :], m.ACC, ACT.Copy).then_inc(acc_copied, 1)

            def step(b, g, first, last):
                s = b * NG + g
                for k in range(KT):
                    for h in range(G):
                        act.wait_ge(scores_made, EXPS * s + G * k + h + 1)
                        if h == 0:
                            act.wait_ge(probs_used, KT * s + k + 1)
                        act.activation(m.probs[k][:, h, :], score_bank(h, last and g >= NG - LEAD), ACT.Exp)\
                            .then_inc(exp_made, 1)
                        if k == 0 and h == G - 1 and not first:
                            copy_output(s - 1)
                    if k == 1 and not (last and g == NG - 1):
                        copy_shift(*after(b, g, 1))
                if last and g == NG - 1:
                    if layer:
                        normalise(None, act, m, rstd_step, root, True, 0, 0, EARLY)
                    copy_output(s)
                    for h in range(CT):
                        act.wait_ge(turned, h + 1)
                        tokens_out(act, m, layer, 0, h).then_inc(tokens_copied, 1)
                    act.wait_ge(tokens_copied, CT)

            groups(act, step)

        @block.vector
        def _(dve):
            def maximum(s, g, j):
                dve.wait_ge(ahead.row_scores_made, MAXES * s + j + 1)
                if j == 0:
                    dve.wait_ge(ahead.shift_made, s - 1)
                dve.tensor_reduce(m.row_max[g % 2][:, j:j + 1], m.max_banks[j % 4], AX.X, ALU.max)\
                    .then_inc(ahead.max_made, 1)

            def negate(s, g, first=False):
                dve.wait_ge(ahead.max_made, MAXES * (s + 1))
                if not first:
                    dve.wait_ge(ahead.shift_turned, s - 1)
                shift_high(dve, m, g % 2).then_inc(ahead.shift_high_made, 1)
                dve.wait_ge(ahead.shift_high_made, s + 1)
                shift_low(dve, m, g % 2).then_inc(ahead.shift_made, 1)

            def write_output(b, g):
                s = b * NG + g
                turned = m.TURN.rearrange("p (q h w) -> p q h w", q=QT, h=G)
                dve.wait_ge(o_turned, 1 + s + 1)
                dve.wait_ge(o_written, 1 + s)
                dve.reciprocal(m.inv_sum[:, :, :, :], turned[:, :, :, DH:DH + 1]).then_inc(inv_made, 1)
                dve.wait_ge(inv_made, s + 1)
                dve.tensor_tensor(m.O[:, bass.ds(b * TPB, TPB), g * G * DH:(g + 1) * G * DH]
                                  .rearrange("p t (h d) -> p t h d", d=DH),
                                  turned[:, :, :, 0:DH], m.inv_sum[:, :, :, :].broadcast_to([P, QT, G, DH]),
                                  ALU.mult).then_inc(o_written, 1)

            def statistics(b):
                dve.wait_ge(o_written, 1 + b * NG + NG)
                for t in range(TPB):
                    dve.bn_stats(m.stats[:, bass.ds(b * TPB + t, 1), :].rearrange("p one s -> p (one s)"),
                                 m.O[:, bass.ds(b * TPB + t, 1), :].rearrange("p one c -> p (one c)"))\
                        .then_inc(stat_step, 1)

            def step(b, g, first, last):
                s = b * NG + g
                more = not (last and g >= NG - LEAD)
                for j in range(MAXES):
                    if more:
                        maximum(s + LEAD, (g + LEAD) % NG, j)
                    if j == 3 * QT + 1 and not first:
                        write_output(*before(b, g))
                if more:
                    negate(s + LEAD, (g + LEAD) % NG)
                if layer and g == 0 and not first:
                    statistics(b - 1)
                if layer and last and g == 2:
                    dve.wait_ge(stat_step, EARLY)
                    for t in range(EARLY):
                        dve.bn_aggr(m.moments[:, t, :], m.stats[:, t, :]).then_inc(stat_step, 1)
                    dve.wait_ge(stat_step, 2 * EARLY)
                    normalise_begin(dve, m, rstd_step, True, 0, 0, EARLY)
                if last and g == NG - 1:
                    if layer:
                        normalise_end(dve, m, rstd_step, root, True, 0, 0, EARLY)
                        for t in range(TPB):
                            normal_tile(dve, m, m.O, t, True).then_inc(tokens_ready, 1)
                    write_output(b, g)
                    if layer:
                        statistics(b)
                        dve.wait_ge(stat_step, NT + EARLY)
                        dve.wait_ge(tokens_ready, TPB)

            negate(1, 1, first=True)
            groups(dve, step)


def turn_batch(nc, m, src, b, turned):
    for h in range(CT):
        for t in range(TPB):
            last = nc.tensor.transpose(m.bank[h][:, t * P:(t + 1) * P],
                                       src[:, TPB * b + t, h * P:(h + 1) * P], m.ident[:, :])
        last.then_inc(turned, 1)


def tokens_out(act, m, layer, b, h):
    if layer:
        return act.activation(m.xT[b % 2][:, h, :], m.bank[h], ACT.Silu,
                              bias=m.mod1_shift[:, h, b:b + 1], scale=m.mod1_scale[:, h, b:b + 1])
    return act.activation(m.xT[b % 2][:, h, :], m.bank[h], ACT.Copy)


def tokens_in(act, m, layer, b, h):
    if layer:
        scale, shift = m.vec[:, NORM_W + h:NORM_W + h + 1], m.vec[:, NORM_B + h:NORM_B + h + 1]
    else:
        scale, shift = m.mod0_scale[:, h, b:b + 1], m.mod0_shift[:, h, b:b + 1]
    return act.activation(m.xT[b % 2][:, h, :], m.bank[h], ACT.Identity, bias=shift, scale=scale)


class Conditioning:
    pass


def conditioning(nc, m, own):
    (vec_turned, vec_ready, cond_turned, cond_ready, es_made, es_copied, es_turned, es_ready, mod_step, mask_step,
     mask_out) = sems(own, nc, "co", "vec_turned", "vec_ready", "cond_turned", "cond_ready", "es_made",
                      "es_copied", "es_turned", "es_ready", "mod_step", "mask_step", "mask_out")
    VEC, ES_TURNED, ES, COND = 4, 5, 6, 7
    c = Conditioning()

    def tensor(pe, part):
        if part == 0:
            nc.tensor.transpose(m.bank[VEC][:, 0:VEC_ROWS], m.vec_rows[:, :], m.ident[0:VEC_ROWS, 0:VEC_ROWS])\
                .then_inc(vec_turned, 1)
            for k in range(KC):
                last = nc.tensor.transpose(m.bank[COND][:, k * B:(k + 1) * B], m.cond_rows[:, k * P:(k + 1) * P],
                                           m.ident[0:B, 0:B])
            last.then_inc(cond_turned, 1)
        elif part == 1:
            pe.wait_ge(cond_ready, 1)
            condition(nc, m, m.bank[ES]).then_inc(es_made, 1)
        elif part == 2:
            pe.wait_ge(es_copied, 1)
            turn_condition(nc, m, m.bank[ES_TURNED]).then_inc(es_turned, 1)

    def scalar(act):
        act.wait_ge(cond_turned, 1)
        act.activation(m.condT[:, :, :], m.bank[COND][:, 0:KC * B].rearrange("p (k b) -> p k b", b=B), ACT.Silu)\
            .then_inc(cond_ready, 1)

    def vector(dve, part):
        if part == 0:
            dve.wait_ge(vec_turned, 1)
            dve.tensor_copy(m.vec[:, :], m.bank[VEC][:, 0:VEC_ROWS]).then_inc(vec_ready, 1)
            dve.tensor_scalar(m.mask_row[:, :], m.mask_row[:, :], -1.0, MASK_VALUE / UNIT, ALU.add, ALU.mult)\
                .then_inc(mask_step, 1)
            dve.wait_ge(mask_step, 1)
            dve.tensor_copy(m.mask_hi[:, :], m.mask_row[:, :]).then_inc(mask_step, 1)
            dve.wait_ge(mask_step, 2)
            dve.tensor_tensor(m.mask_lo[:, :], m.mask_row[:, :], m.mask_hi[:, :], ALU.subtract).then_inc(mask_step, 1)
        elif part == 2:
            dve.wait_ge(es_made, 1)
            dve.tensor_copy(m.ss_rows[:, :], m.bank[ES][0:B, :]).then_inc(es_copied, 1)
        elif part == 3:
            dve.wait_ge(es_turned, 1)
            dve.tensor_copy(m.es[:, :, :], m.bank[ES_TURNED][:, 0:KC * B].rearrange("p (k b) -> p k b", b=B))\
               .then_inc(es_ready, 1)
            dve.wait_ge(es_ready, 1)

    def gpsimd(pool):
        pool.wait_ge(vec_ready, 1)
        pool.wait_ge(es_ready, 1)
        for k in range(KC):
            pool.tensor_scalar(m.mod1[:, k, :], m.es[:, k, :], m.vec[:, EMB_B + k:EMB_B + k + 1],
                               1.0 if k < CT else 0.0, ALU.add, ALU.add).then_inc(mod_step, 1)
        pool.wait_ge(mod_step, KC)
        for h in range(CT):
            pool.tensor_scalar(m.mod1_scale[:, h, :], m.mod1[:, h, :], m.vec[:, SBN_W + h:SBN_W + h + 1], None,
                               ALU.mult).then_inc(mod_step, 1)
            pool.tensor_scalar(m.mod1_shift[:, h, :], m.mod1[:, h, :], m.vec[:, SBN_B + h:SBN_B + h + 1], None,
                               ALU.mult).then_inc(mod_step, 1)
        pool.wait_ge(mod_step, KC + 2 * CT)
        pool.tensor_tensor(m.mod1_shift[:, :, :], m.mod1_shift[:, :, :], m.mod1[:, CT:2 * CT, :], ALU.add)\
            .then_inc(mod_step, 1)
        pool.wait_ge(mod_step, KC + 2 * CT + 1)

    def sync(sp):
        sp.wait_ge(mask_step, 3)
        sp.dma_start(m.mask_dram[0], m.mask_hi[:, :]).then_inc(mask_out, 16)
        sp.dma_start(m.mask_dram[1], m.mask_lo[:, :]).then_inc(mask_out, 16)
        sp.wait_ge(mask_out, 32)

    c.vec_ready, c.cond_ready = vec_ready, cond_ready
    c.tensor, c.scalar, c.vector, c.gpsimd, c.sync = tensor, scalar, vector, gpsimd, sync
    return c


def finish(nc, layer, m):
    w = m.wo1 if layer else m.wo
    with ExitStack() as own:
        (step, root, mean_made, src_ready, turned, srcT_ready, y_made, y_added, stat_step, y_out) = sems(
            own, nc, f"fi{layer}", "step", "root", "mean_made", "src_ready", "turned", "srcT_ready", "y_made", "y_added",
            "stat_step", "y_out")

        def y_bank(t):
            return m.bank[(2, 3, 4, 7)[t % Y_BANKS]]

        Y_BANKS = 4
        cond = None if layer else conditioning(nc, m, own)
        block = own.enter_context(nc.Block())
        src = m.XN if layer else m.O

        @block.gpsimd
        def _(pool):
            if not layer:
                cond.gpsimd(pool)

        @block.vector
        def _(dve):
            if layer:
                for t in range(EARLY, NT):
                    dve.bn_aggr(m.moments[:, t, :], m.stats[:, t, :]).then_inc(stat_step, 1)
                dve.wait_ge(stat_step, NT - EARLY)
                normalise_begin(dve, m, step, True, 0, EARLY, NT)
                for t in range(TPB, EARLY):
                    normal_tile(dve, m, m.O, t, True).then_inc(src_ready, 1)
            for t in range(NT):
                if layer and t == TPB:
                    normalise_end(dve, m, step, root, True, 0, EARLY, NT)
                    for u in range(EARLY, NT):
                        normal_tile(dve, m, m.O, u, True).then_inc(src_ready, 1)
                if not layer and t % TPB == 0:
                    cond.vector(dve, t // TPB)
                dve.wait_ge(y_made, t + 1)
                dve.tensor_tensor(m.X[:, t, :], y_bank(t)[:, 0:C], m.X[:, t, :], ALU.add).then_inc(y_added, 1)
                if not layer and t < NT - TPB:
                    dve.wait_ge(y_added, t + 1)
                    dve.bn_stats(m.stats[:, t, :], m.X[:, t, :]).then_inc(stat_step, 1)
                    if t == FIRST:
                        dve.wait_ge(stat_step, FIRST + 1)
                        for u in range(FIRST):
                            dve.bn_aggr(m.moments[:, u, :], m.stats[:, u, :]).then_inc(stat_step, 1)
                        dve.wait_ge(stat_step, 2 * FIRST + 1)
                        normalise_begin(dve, m, step, True, 0, 0, FIRST)
                    if t == FIRST + 3:
                        normalise_end(dve, m, step, root, True, 0, 0, FIRST)
                        dve.scalar_tensor_tensor(m.mean_rstd[:, :], m.moments[:, 0:FIRST, 0], -1.0, m.rstd[:, 0:FIRST],
                                                 ALU.mult, ALU.mult).then_inc(mean_made, 1)
            if not layer:
                dve.wait_ge(stat_step, NT - TPB + FIRST)
                dve.wait_ge(y_added, NT)

        @block.scalar
        def _(act):
            act.sem_inc(turned, CT)
            act.sem_inc(srcT_ready, CT)
            if not layer:
                cond.scalar(act)
            for b in range(1, B):
                for h in range(CT):
                    act.wait_ge(turned, CT * b + h + 1)
                    if b >= 2:
                        act.wait_ge(y_made, TPB * (b - 1))
                    tokens_out(act, m, layer, b, h).then_inc(srcT_ready, 1)
                if layer and b == 1:
                    normalise(None, act, m, step, root, True, 0, EARLY, NT)
                if not layer and b == 2:
                    normalise(None, act, m, step, root, True, 0, 0, FIRST)
                    act.wait_ge(mean_made, 1)
                    for t in range(FIRST):
                        act.activation(m.XN[:, t, :], m.X[:, t, :], ACT.Identity, bias=m.mean_rstd[:, t:t + 1],
                                       scale=m.rstd[:, t:t + 1]).then_inc(src_ready, 1)
            if not layer:
                for h in range(CT):
                    act.wait_ge(turned, CT * B + h + 1)
                    act.wait_ge(y_made, TPB * (B - 1))
                    tokens_in(act, m, 1, 0, h).then_inc(srcT_ready, 1)
                act.wait_ge(src_ready, FIRST)
                act.wait_ge(srcT_ready, CT * (B + 1))

        @block.tensor
        def _(pe):
            def turn(b):
                for h in range(CT):
                    pe.wait_ge(srcT_ready, CT * (b - 1) + h + 1)
                    for t in range(TPB):
                        if layer:
                            pe.wait_ge(src_ready, TPB * (b - 1) + t + 1)
                        last = nc.tensor.transpose(m.bank[h][:, t * P:(t + 1) * P],
                                                   src[:, TPB * b + t, h * P:(h + 1) * P], m.ident[:, :])
                    last.then_inc(turned, 1)

            if not layer:
                cond.tensor(pe, 0)
            for b in range(B):
                for t in range(TPB):
                    n = TPB * b + t
                    if not layer and b and t == 2:
                        cond.tensor(pe, b)
                    if t == 2 and b + 1 < B:
                        turn(b + 1)
                    if not layer and n == 2:
                        pe.wait_ge(cond.vec_ready, 1)
                        pe.wait_ge(cond.cond_ready, 1)
                    if n >= Y_BANKS:
                        pe.wait_ge(y_added, n - Y_BANKS + 1)
                    for k in range(CT):
                        if t == 0:
                            pe.wait_ge(srcT_ready, CT * b + k + 1)
                        last = nc.tensor.matmul(y_bank(n)[:, 0:C], m.xT[b % 2][:, k, t * P:(t + 1) * P],
                                                w[:, k, :], start=(k == 0), stop=(k == CT - 1))
                    last.then_inc(y_made, 1)
            if not layer:
                pe.wait_ge(srcT_ready, CT * B)
                pe.wait_ge(src_ready, TPB)
                turn_batch(nc, m, m.XN, 0, turned)

        @block.sync
        def _(sp):
            if not layer:
                cond.sync(sp)
            if layer:
                steps = [(t, 2) for t in range(0, NT - 2, 2)] + [(NT - 2, 1), (NT - 1, 1)]
                for t, tiles in steps:
                    b, q = divmod(t, TPB)
                    sp.wait_ge(y_added, t + tiles)
                    sp.dma_start(m.out[b, q * P:(q + tiles) * P, :].rearrange("(t p) c -> p t c", p=P),
                                 m.X[:, t:t + tiles, :]).then_inc(y_out, 16)
                sp.wait_ge(y_out, 16 * len(steps))


_INS = ["x", "cond_2048", "mask_BxS_ff1", "L0_cond_pos", "L0_cond_rms_w", "L0_cond_w_cond", "L0_cond_w_qkv",
        "L0_cond_w_out",
        "L1_cond_norm_w", "L1_cond_norm_b", "L1_cond_q_w", "L1_cond_q_b", "L1_cond_k_w", "L1_cond_k_b",
        "L1_cond_v_w", "L1_cond_v_b", "L1_cond_emb_w", "L1_cond_emb_b", "L1_cond_sb_norm_w",
        "L1_cond_sb_norm_b", "L1_cond_out_w", "L1_cond_out_b"]


def kernel(**inputs):
    import numpy as np
    import concourse.bacc as bacc
    from concourse.bass_utils import run_bass_kernel_spmd

    nc = bacc.Bacc("TRN2", target_bir_lowering=False, num_devices=1)
    arrays, args = {}, []
    for name in _INS:
        a = np.ascontiguousarray(inputs[name])
        arrays[f"in_{name}"] = a
        args.append(nc.dram_tensor(f"in_{name}", a.shape, mybir.dt.from_np(a.dtype), kind="ExternalInput").ap())
    args.append(nc.dram_tensor("y", (B, S, C), F32, kind="ExternalOutput").ap())
    build(nc, *args)
    r = run_bass_kernel_spmd(nc, [arrays], core_ids=[0])
    return r.results[0]["y"]
```
